# Optimizing a Trainium2 kernel written in Bass

```python
import numpy as np
import jax
import jax.numpy as jnp

def _softmax(x, axis=-1):
    return jax.nn.softmax(x, axis=axis)

def _gelu(x):
    return jax.nn.gelu(x, approximate=True)

def _silu(x):
    return jax.nn.silu(x)

def _sigmoid(x):
    return jax.nn.sigmoid(x)

def _layernorm(x, axis=-1, eps=1e-05):
    m = jnp.mean(x, axis=axis, keepdims=True)
    v = jnp.var(x, axis=axis, keepdims=True)
    return (x - m) / jnp.sqrt(v + eps)

def _scatter_add(tgt, idx, src, axis=0):
    return tgt.at[idx].add(src)

def _segment_sum(src, seg, n):
    return jax.ops.segment_sum(src, seg, n)
kernel_name = 'mk_xattn_ffn_d1_seqx_r8_33f476'

def setup_inputs(seed: int=0):
    np.random.seed(seed)
    _w = jnp.asarray

    def _rec_inputs():
        import jax
        import jax.numpy as jnp
        _rk = jax.random.key(seed)
        x = -0.0002928 + 1 * jax.random.normal(jax.random.fold_in(_rk, 1), (2, 256, 128), jnp.float32)
        _lenS = 256 - jax.random.randint(jax.random.fold_in(_rk, 7), (2,), 0, max(1, 256 // 4) + 1, jnp.int32)
        _lenS2 = 512 - jax.random.randint(jax.random.fold_in(_rk, 8), (2,), 0, max(1, 512 // 4) + 1, jnp.int32)
        _ctx_1024P = jax.random.normal(jax.random.fold_in(_rk, 11), (2, 16, 128), jnp.float32)
        _ctx_1024c = jax.random.dirichlet(jax.random.fold_in(_rk, 511), 0.3 * jnp.ones((16,), jnp.float32), (2, 512))
        _ctx_1024t = jnp.einsum('bsk,bkd->bsd', _ctx_1024c, _ctx_1024P)
        _ctx_1024t = _ctx_1024t * jax.lax.rsqrt(jnp.mean(jnp.square(_ctx_1024t)) + 1e-12) * 0.953939
        ctx_1024 = -1.39393e-06 + 0.999914 * (_ctx_1024t + 0.3 * jax.random.normal(jax.random.fold_in(_rk, 611), (2, 512, 128), jnp.float32))
        return (x, ctx_1024)
    x, ctx_1024 = _rec_inputs()

    def _L0_xattn_setup():
        import jax, jax.numpy as jnp
        import numpy as np
        B, S, D, DV = (1, 512, 128, 128)
        key = jax.random.key(seed)
        kq, kk, kv, ks, kp = jax.random.split(key, 5)
        return {'q': jax.random.normal(kq, (B, S, D), dtype=jnp.float32), 'k': jax.random.normal(kk, (B, S, D), dtype=jnp.float32), 'v': jax.random.normal(kv, (B, S, DV), dtype=jnp.float32), 'scale_factor': jax.random.normal(ks, (1,), dtype=jnp.float32), 'dropout_p': jax.random.uniform(kp, (1,), dtype=jnp.float32)}
    _L0_xattn_all = _L0_xattn_setup()
    _L0_xattn_in = {k: v for k, v in _L0_xattn_all.items() if k in ('scale_factor', 'dropout_p')}
    del _L0_xattn_all

    def _L0_ffn_setup():
        import jax, jax.numpy as jnp
        import numpy as np
        TOP_K = 2
        EPS = 1e-05

        def layer_norm(x, g, b):
            mu = jnp.mean(x, axis=-1, keepdims=True)
            var = jnp.mean(jnp.square(x - mu), axis=-1, keepdims=True)
            return (x - mu) * jax.lax.rsqrt(var + EPS) * g + b
        key = jax.random.key(seed)
        ks = jax.random.split(key, 12)
        B, S, D, F, E = (2, 256, 128, 512, 8)
        std = 0.02
        return {'x': jax.random.normal(ks[0], (B, S, D), jnp.float32), 'g1': jnp.ones((D,), jnp.float32), 'be1': jnp.zeros((D,), jnp.float32), 'mix_w': jax.random.normal(ks[1], (D, D), jnp.float32) * std, 'mix_b': jnp.zeros((D,), jnp.float32), 'g2': jnp.ones((D,), jnp.float32), 'be2': jnp.zeros((D,), jnp.float32), 'router_w': jax.random.normal(ks[2], (D, E), jnp.float32) * std, 'w1': jax.random.normal(ks[3], (E, D, F), jnp.float32) * std, 'b1': jnp.zeros((E, F), jnp.float32), 'w2': jax.random.normal(ks[4], (E, F, D), jnp.float32) * std, 'b2': jnp.zeros((E, D), jnp.float32)}
    _L0_ffn_all = _L0_ffn_setup()
    _L0_ffn_in = {k: v for k, v in _L0_ffn_all.items() if k in ('g1', 'be1', 'mix_w', 'mix_b', 'g2', 'be2', 'router_w', 'w1', 'b1', 'w2', 'b2')}
    del _L0_ffn_all
    return {'x': x, 'ctx_1024': ctx_1024, 'L0_xattn_scale_factor': _L0_xattn_in['scale_factor'], 'L0_xattn_dropout_p': _L0_xattn_in['dropout_p'], 'L0_ffn_g1': _L0_ffn_in['g1'], 'L0_ffn_be1': _L0_ffn_in['be1'], 'L0_ffn_mix_w': _L0_ffn_in['mix_w'], 'L0_ffn_mix_b': _L0_ffn_in['mix_b'], 'L0_ffn_g2': _L0_ffn_in['g2'], 'L0_ffn_be2': _L0_ffn_in['be2'], 'L0_ffn_router_w': _L0_ffn_in['router_w'], 'L0_ffn_w1': _L0_ffn_in['w1'], 'L0_ffn_b1': _L0_ffn_in['b1'], 'L0_ffn_w2': _L0_ffn_in['w2'], 'L0_ffn_b2': _L0_ffn_in['b2']}

def reference(x, ctx_1024, L0_xattn_scale_factor, L0_xattn_dropout_p, L0_ffn_g1, L0_ffn_be1, L0_ffn_mix_w, L0_ffn_mix_b, L0_ffn_g2, L0_ffn_be2, L0_ffn_router_w, L0_ffn_w1, L0_ffn_b1, L0_ffn_w2, L0_ffn_b2):
    import jax
    import jax.numpy as jnp

    def _L0_xattn_ref(q, k, v, scale_factor, dropout_p):
        import jax, jax.numpy as jnp
        import numpy as np
        B, S, D, DV = (1, 512, 128, 128)
        b, s, d = q.shape
        step = s // 4
        scale = q[:, ::step].reshape(b, -1)
        qk = jnp.einsum('bsd,btd->bst', q, k)
        scaled_qk = qk * scale[:, None, :]
        softmax_qk = jax.nn.softmax(scaled_qk, axis=-1)
        return jnp.einsum('bst,btv->bsv', softmax_qk, v)

    def _L0_ffn_ref(x, g1, be1, mix_w, mix_b, g2, be2, router_w, w1, b1, w2, b2):
        import jax, jax.numpy as jnp
        import numpy as np
        TOP_K = 2
        EPS = 1e-05

        def layer_norm(x, g, b):
            mu = jnp.mean(x, axis=-1, keepdims=True)
            var = jnp.mean(jnp.square(x - mu), axis=-1, keepdims=True)
            return (x - mu) * jax.lax.rsqrt(var + EPS) * g + b
        res = x
        n = layer_norm(x, g1, be1)
        x = res + n + (n @ mix_w + mix_b)
        res = x
        n = layer_norm(x, g2, be2)
        B, S, D = n.shape
        E = w1.shape[0]
        flat = n.reshape(-1, D)
        probs = jax.nn.softmax(flat @ router_w, axis=-1)
        topw, topi = jax.lax.top_k(probs, TOP_K)
        combine = jnp.sum(jax.nn.one_hot(topi, E, dtype=flat.dtype) * topw[..., None], axis=1)
        h = jax.nn.silu(jnp.einsum('td,edf->tef', flat, w1) + b1)
        y = jnp.einsum('tef,efd->ted', h, w2) + b2
        out = jnp.einsum('te,ted->td', combine, y)
        return res + out.reshape(B, S, D)
    x = x + _L0_xattn_ref(_layernorm(x, axis=-1), ctx_1024, ctx_1024, L0_xattn_scale_factor, L0_xattn_dropout_p)
    x = x + _L0_ffn_ref(_layernorm(x, axis=-1), L0_ffn_g1, L0_ffn_be1, L0_ffn_mix_w, L0_ffn_mix_b, L0_ffn_g2, L0_ffn_be2, L0_ffn_router_w, L0_ffn_w1, L0_ffn_b1, L0_ffn_w2, L0_ffn_b2)
    return x

_drawn_inputs = setup_inputs


def setup_inputs(seed=0):
    import zlib

    import numpy as np

    out = dict(_drawn_inputs(seed))
    spreads = {'L0_ffn_g1': (1.0, 0.2),
     'L0_ffn_be1': (0.0, 0.1),
     'L0_ffn_mix_b': (0.0, 0.269),
     'L0_ffn_g2': (1.0, 0.6),
     'L0_ffn_be2': (0.0, 0.8),
     'L0_ffn_b1': (0.0, 0.8),
     'L0_ffn_b2': (0.0, 0.8)}
    factors = {'L0_ffn_router_w': 8.0, 'L0_ffn_w1': 8.0, 'L0_ffn_w2': 8.0}
    for name, (base, spread) in spreads.items():
        noise = np.random.default_rng([zlib.crc32(name.encode()), seed]).standard_normal(out[name].shape)
        drawn = base * np.exp(spread * noise) if base else spread * noise
        out[name] = jnp.asarray(drawn.astype(out[name].dtype))
    for name, factor in factors.items():
        out[name] = (out[name] * factor).astype(out[name].dtype)
    return out
```

```python
from contextlib import ExitStack

import concourse.bass as bass
from concourse import mybir

F32 = mybir.dt.float32
F32R = mybir.dt.float32r
I32 = mybir.dt.int32
ALU = mybir.AluOpType
ACT = mybir.ActivationFunctionType
AX_X = mybir.AxisListType.X

P = 128
EPS = 1e-5
TOP_K = 2
RSQRT_GUESS = float(0x5F3759DF)
NEWTON_STEPS = 3


def xattn_moe_kernel(nc: bass.Bass, x, ctx_kv, g1, be1, mix_w, mix_b, g2, be2, router_w, w1, b1, w2, b2, out):
    B, S, D = x.shape
    SK = ctx_kv.shape[1]
    E, _, F = w1.shape
    T = B * S // P
    TB = S // P
    KC = SK // P
    FC = F // P
    N = B * S
    STEP = S // 4
    assert D == P and KC == 4 and N == 512 and B == 2

    NCH = E * FC
    H_BANKS = 3
    H_BUFS = 4
    LAG = 3
    ROWS = NCH + 4

    x_tok = x.rearrange("b (n p) d -> p (b n) d", p=P)
    out_tok = out.rearrange("b (n p) d -> p (b n) d", p=P)
    kv_tok = ctx_kv.rearrange("b (n p) d -> b p n d", p=P)
    w1_view = w1.rearrange("e d f -> d e f")
    w2_view = w2.rearrange("e (c p) d -> p e c d", p=P)
    weight_rows = nc.dram_tensor("weight_rows", [E, N], F32, kind="Internal").ap()

    with ExitStack() as stack:
        def sb(name, shape, dt=F32):
            return stack.enter_context(nc.sbuf_tensor(name, shape, dt))

        def sem(name):
            return stack.enter_context(nc.semaphore(name))

        bank = [stack.enter_context(nc.psum_tensor(f"bank{i}", [P, 512], F32)) for i in range(8)]
        qT_ps, const_ps, kT_ps = [bank[0], bank[1]], bank[2], [bank[3], bank[4]]
        score_ps = [bank[5], bank[6], bank[7], bank[0]]
        pT_ps = [(bank[1], bank[2]), (bank[3], bank[4]), (bank[5], bank[6]), (bank[7], bank[0])]
        attn_ps = [bank[1], bank[3], bank[5], bank[7]]
        n1T_ps, mix_ps = [bank[2], bank[4]], [bank[6], bank[1], bank[3], bank[0]]
        n2T_ps, logit_ps = [bank[5], bank[7]], bank[2]
        hid_ps, y_ps = [bank[6], bank[1], bank[3]], [bank[0], bank[4]]
        rowsT_ps, b2_ps, outT_ps = bank[5], bank[7], [bank[2], bank[5]]

        ident = sb("ident", [P, P])
        xs = sb("xs", [P, T, D])
        kv = sb("kv", [P, B, KC, D])
        const_rows = sb("const_rows", [ROWS, P])
        const_cols = sb("const_cols", [P, ROWS])
        mixw = sb("mixw", [P, D])
        mixwi = sb("mixwi", [P, D])
        mixb = sb("mixb", [P, D])
        routw = sb("routw", [P, E])
        b2s = sb("b2s", [E, D])
        w1s = sb("w1s", [P, E, F])
        w2s = sb("w2s", [P, E, FC, D])
        w1h = sb("w1h", [P, E, F], F32R)
        w1l = sb("w1l", [P, E, F], F32R)
        w2h = sb("w2h", [P, E, FC, D], F32R)
        w2l = sb("w2l", [P, E, FC, D], F32R)

        stats = sb("stats", [P, T, 6])
        meanvar = sb("meanvar", [P, T, 2])
        var_eps = sb("var_eps", [P, 8])
        half_bits = sb("half_bits", [P, 8], I32)
        newton = sb("newton", [P, 8])
        rstd = sb("rstd", [P, 8])
        qn = sb("qn", [P, T, D])
        qT = sb("qT", [P, N])
        ks = sb("ks", [P, B, KC, D])
        kT = sb("kT", [P, B, SK])
        negmax = sb("negmax", [P, T])
        probs = sb("probs", [P, T, SK])
        probsum = sb("probsum", [P, T])
        probrec = sb("probrec", [P, T])
        pT = sb("pT", [P, T, SK])
        x1 = sb("x1", [P, T, D])
        z = sb("z", [P, T, D])
        zb = sb("zb", [P, T, D])
        u1 = sb("u1", [P, T, D])
        n1T = sb("n1T", [P, N])
        x2 = sb("x2", [P, T, D])
        u2 = sb("u2", [P, T, D])
        resid = sb("resid", [P, T, D])
        n2T = sb("n2T", [P, N])
        n2h = sb("n2h", [P, N], F32R)
        n2l = sb("n2l", [P, N], F32R)

        negtop = sb("negtop", [P, T])
        lshift = sb("lshift", [P, T, E])
        gate = sb("gate", [P, T, 2 * E])
        gate_rest = sb("gate_rest", [P, T, 2 * E])
        gate_sum = sb("gate_sum", [P, T])
        gate_rec = sb("gate_rec", [P, T])
        top8 = sb("top8", [P, T, 8])
        wanted = sb("wanted", [P, T, 8])
        picked = sb("picked", [P, T, E])
        weight = sb("weight", [P, T, E])
        weightT = sb("weightT", [E, N])
        weight_all = sb("weight_all", [P, E, N])

        hid = sb("hid", [P, H_BUFS, N])
        hidh = sb("hidh", [P, H_BUFS, N], F32R)
        hidl = sb("hidl", [P, H_BUFS, N], F32R)
        y_part = sb("y_part", [P, 2, N])
        acc = sb("acc", [P, N])
        result = sb("result", [P, T, D])
        warm = sb("warm", [P, 1])

        x_in, kv_in, out_done = sem("x_in"), [sem("kv_in0"), sem("kv_in1")], sem("out_done")
        rows_in, mixw_in, mixb_in, routw_in, b2_in = (sem(n) for n in ("rows_in", "mixw_in", "mixb_in", "routw_in", "b2_in"))
        w1_in = [sem(f"w1_in{e}") for e in range(E)]
        w2_in = [sem(f"w2_in{e}") for e in range(E)]
        zero_done, ident_ready, mixwi_ready, warm_set = (sem(n) for n in ("zero_done", "ident_ready", "mixwi_ready", "warm_set"))
        const_tp, const_ready = sem("const_tp"), sem("const_ready")
        dve_step = sem("dve_step")
        qn_ready, qT_tp, qT_ready, ks_ready, kT_tp, kT_ready = (sem(n) for n in ("qn_ready", "qT_tp", "qT_ready", "ks_ready", "kT_tp", "kT_ready"))
        score_ready, negmax_ready, prob_ready, pT_tp, pT_act, pT_dve, attn_ready, x1_ready = (
            sem(n) for n in ("score_ready", "negmax_ready", "prob_ready", "pT_tp", "pT_act", "pT_dve", "attn_ready", "x1_ready"))
        u1_ready, z_ready, zb_ready, u1_tp, n1T_ready, mix_ready, x2_ready = (
            sem(n) for n in ("u1_ready", "z_ready", "zb_ready", "u1_tp", "n1T_ready", "mix_ready", "x2_ready"))
        u2_ready, u2_tp, n2T_ready, n2h_ready, n2l_ready, resid_ready = (
            sem(n) for n in ("u2_ready", "u2_tp", "n2T_ready", "n2h_ready", "n2l_ready", "resid_ready"))
        logit_ready, lshift_ready, gate_ready, pads_ready, weight_ready, weightT_tp, weightT_ready = (
            sem(n) for n in ("logit_ready", "lshift_ready", "gate_ready", "pads_ready", "weight_ready", "weightT_tp", "weightT_ready"))
        rows_out, spread_in, b2_ready = sem("rows_out"), [sem(f"spread_in{e}") for e in range(E)], sem("b2_ready")
        w1h_ready, w2h_ready, w1l_ready, w2l_ready = (sem(n) for n in ("w1h_ready", "w2h_ready", "w1l_ready", "w2l_ready"))
        hid_mm, hid_ready, hidh_ready, hidl_ready, hid_used, y_part_ready, acc_ready = (
            sem(n) for n in ("hid_mm", "hid_ready", "hidh_ready", "hidl_ready", "hid_used", "y_part_ready", "acc_ready"))
        acc_tp, result_ready = sem("acc_tp"), sem("result_ready")

        block = stack.enter_context(nc.Block())

        @block.sync
        def _(sp):
            sp.dma_start(xs[:], x_tok).then_inc(x_in, 16)
            sp.dma_start(kv[:, 0], kv_tok[0]).then_inc(kv_in[0], 16)
            sp.dma_start(kv[:, 1], kv_tok[1]).then_inc(kv_in[1], 16)
            sp.dma_start(const_rows[0:NCH, :], b1.rearrange("e (c p) -> (e c) p", p=P)).then_inc(rows_in, 16)
            for i, v in enumerate((g1, be1, g2, be2)):
                sp.dma_start(const_rows[NCH + i:NCH + i + 1, :], v.rearrange("(o d) -> o d", o=1)).then_inc(rows_in, 16)
            sp.dma_start(mixw[:], mix_w).then_inc(mixw_in, 16)
            sp.dma_start(mixb[:], mix_b.partition_broadcast(P)).then_inc(mixb_in, 16)
            sp.dma_start(routw[:], router_w).then_inc(routw_in, 16)
            sp.dma_start(b2s[:], b2).then_inc(b2_in, 16)
            for e in range(E):
                sp.dma_start(w1s[:, e], w1_view[:, e]).then_inc(w1_in[e], 16)
                sp.dma_start(w2s[:, e], w2_view[:, e]).then_inc(w2_in[e], 16)
            sp.wait_ge(weightT_ready, 1)
            sp.dma_start(weight_rows, weightT[:]).then_inc(rows_out, 16)
            sp.wait_ge(rows_out, 16)
            for e in range(E):
                sp.dma_start(weight_all[:, e, :], weight_rows[e, :].partition_broadcast(P)).then_inc(spread_in[e], 16)
            for half in range(2):
                sp.wait_ge(result_ready, half + 1)
                sp.dma_start(out_tok[:, 2 * half:2 * half + 2], result[:, 2 * half:2 * half + 2]).then_inc(out_done, 16)
            sp.wait_ge(out_done, 32)

        @block.gpsimd
        def _(pool):
            nc.gpsimd.memset(ident[:], 0.0).then_inc(zero_done, 1)
            pool.wait_ge(zero_done, 1)
            nc.gpsimd.affine_select(out=ident[:], in_=ident[:], compare_op=ALU.not_equal, fill=1.0, base=0,
                                    pattern=[[-1, P]], channel_multiplier=1).then_inc(ident_ready, 1)
            pool.wait_ge(ident_ready, 1)
            pool.wait_ge(mixw_in, 16)
            nc.gpsimd.tensor_tensor(mixwi[:], mixw[:], ident[:], ALU.add).then_inc(mixwi_ready, 1)

            def low_parts(e):
                pool.wait_ge(w1h_ready, e + 1)
                nc.gpsimd.tensor_tensor(w1l[:, e], w1s[:, e], w1h[:, e].bitcast(F32), ALU.subtract).then_inc(w1l_ready, 1)
                pool.wait_ge(w2h_ready, e + 1)
                nc.gpsimd.tensor_tensor(w2l[:, e], w2s[:, e], w2h[:, e].bitcast(F32), ALU.subtract).then_inc(w2l_ready, 1)

            low_parts(0)
            pool.wait_ge(mixb_in, 16)
            for i in range(T):
                pool.wait_ge(z_ready, i + 1)
                nc.gpsimd.tensor_tensor(zb[:, i], z[:, i], mixb[:], ALU.add).then_inc(zb_ready, 1)
            low_parts(1)
            for i in range(T):
                pool.wait_ge(x2_ready, i + 1)
                nc.gpsimd.tensor_tensor(resid[:, i], x1[:, i], x2[:, i], ALU.add).then_inc(resid_ready, 1)
            for e in range(E):
                if e + 2 < E:
                    low_parts(e + 2)
                if 0 < e < E - 1:
                    pool.wait_ge(y_part_ready, e + 1)
                    pool.wait_ge(acc_ready, e)
                    nc.gpsimd.tensor_tensor(acc[:], acc[:], y_part[:, e % 2], ALU.add).then_inc(acc_ready, 1)

        @block.scalar
        def _(act):
            act.wait_ge(warm_set, 1)
            nc.scalar.activation(warm[:], warm[:], ACT.Exp)
            for b in range(B):
                act.wait_ge(qT_tp, b + 1)
                nc.scalar.copy(qT[:, b * S:(b + 1) * S], qT_ps[b][:, 0:S]).then_inc(qT_ready, 1)
            act.wait_ge(const_tp, 1)
            nc.scalar.copy(const_cols[:], const_ps[:, 0:ROWS]).then_inc(const_ready, 1)
            for b in range(B):
                act.wait_ge(kT_tp, b + 1)
                nc.scalar.copy(kT[:, b], kT_ps[b][:]).then_inc(kT_ready, 1)

            def half_pT(i):
                act.wait_ge(pT_tp, i + 1)
                nc.scalar.copy(pT[:, i, 0:256], pT_ps[i][0][:, 0:256]).then_inc(pT_act, 1)

            for i in range(T):
                act.wait_ge(negmax_ready, i + 1)
                nc.scalar.activation(probs[:, i], score_ps[i][:], ACT.Exp, bias=negmax[:, i:i + 1],
                                     accum_out=probsum[:, i:i + 1]).then_inc(prob_ready, 1)
                if i:
                    half_pT(i - 1)
            half_pT(T - 1)
            for b in range(B):
                act.wait_ge(u1_tp, b + 1)
                if b == 0:
                    act.wait_ge(const_ready, 1)
                cols = slice(b * S, (b + 1) * S)
                nc.scalar.activation(n1T[:, cols], n1T_ps[b][:, 0:S], ACT.Identity, bias=const_cols[:, NCH + 1:NCH + 2],
                                     scale=const_cols[:, NCH:NCH + 1]).then_inc(n1T_ready, 1)
            for b in range(B):
                act.wait_ge(u2_tp, b + 1)
                cols = slice(b * S, (b + 1) * S)
                nc.scalar.activation(n2T[:, cols], n2T_ps[b][:, 0:S], ACT.Identity, bias=const_cols[:, NCH + 3:NCH + 4],
                                     scale=const_cols[:, NCH + 2:NCH + 3]).then_inc(n2T_ready, 1)
            act.wait_ge(lshift_ready, 1)
            act.wait_ge(pads_ready, 1)
            nc.scalar.activation(gate[:, :, 0:E], lshift[:], ACT.Exp).then_inc(gate_ready, 1)

            def silu(n):
                act.wait_ge(hid_mm, n + 1)
                if n >= H_BUFS:
                    act.wait_ge(hidl_ready, n - H_BUFS + 1)
                nc.scalar.activation(hid[:, n % H_BUFS], hid_ps[n % H_BANKS][:], ACT.Silu,
                                     bias=const_cols[:, n:n + 1]).then_inc(hid_ready, 1)

            def high_part(n):
                act.wait_ge(hid_ready, n + 1)
                if n >= H_BUFS:
                    act.wait_ge(hid_used, n - H_BUFS + 1)
                nc.scalar.copy(hidh[:, n % H_BUFS], hid[:, n % H_BUFS]).then_inc(hidh_ready, 1)

            for n in range(NCH):
                silu(n)
                if n:
                    high_part(n - 1)
            high_part(NCH - 1)

        @block.vector
        def _(dve):
            steps = [0]

            def then(ins):
                steps[0] += 1
                ins.then_inc(dve_step, 1)
                dve.wait_ge(dve_step, steps[0])

            def row_stats(src, i):
                nc.vector.bn_stats(stats[:, i], src[:, i]).then_inc(dve_step, 1)
                steps[0] += 1

            def aggregate(tiles):
                dve.wait_ge(dve_step, steps[0])
                for i in tiles:
                    nc.vector.bn_aggr(meanvar[:, i], stats[:, i]).then_inc(dve_step, 1)
                    steps[0] += 1
                dve.wait_ge(dve_step, steps[0])

            def rsqrt(n):
                v, y, t = var_eps[:, 0:n], rstd[:, 0:n], newton[:, 0:n]
                then(nc.vector.tensor_scalar(half_bits[:, 0:n], v.bitcast(I32), 1, None, ALU.logical_shift_right))
                then(nc.vector.tensor_scalar(y.bitcast(I32), half_bits[:, 0:n], -1.0, RSQRT_GUESS, ALU.mult, ALU.add))
                for _ in range(NEWTON_STEPS):
                    then(nc.vector.tensor_tensor(t, y, y, ALU.mult))
                    then(nc.vector.scalar_tensor_tensor(out=t, in0=t, scalar=-0.5, in1=v, op0=ALU.mult, op1=ALU.mult))
                    then(nc.vector.scalar_tensor_tensor(out=y, in0=t, scalar=1.5, in1=y, op0=ALU.add, op1=ALU.mult))

            def normalized(dst, src, i, col):
                return nc.vector.tensor_scalar(dst[:, i], src[:, i], meanvar[:, i, 0:1], rstd[:, col:col + 1],
                                               ALU.subtract, ALU.mult)

            def weight_high(e):
                dve.wait_ge(w1_in[e], 16)
                nc.vector.tensor_copy(w1h[:, e], w1s[:, e]).then_inc(w1h_ready, 1)
                dve.wait_ge(w2_in[e], 16)
                nc.vector.tensor_copy(w2h[:, e], w2s[:, e]).then_inc(w2h_ready, 1)

            nc.vector.memset(warm[:], 0.0).then_inc(warm_set, 1)
            nc.vector.memset(gate[:], -1.0).then_inc(pads_ready, 1)
            then(nc.vector.memset(wanted[:], -1.0))

            dve.wait_ge(x_in, 16)
            for i in range(T):
                row_stats(xs, i)
            aggregate(range(T))
            then(nc.vector.tensor_scalar(var_eps[:, 0:T], meanvar[:, :, 1], EPS, None, ALU.add))
            rsqrt(T)
            for i in range(T):
                normalized(qn, xs, i, i).then_inc(qn_ready, 1)
            for b in range(B):
                dve.wait_ge(qT_ready, b + 1)
                dve.wait_ge(kv_in[b], 16)
                for j in range(KC):
                    col = b * S + STEP * j
                    nc.vector.tensor_scalar(ks[:, b, j], kv[:, b, j], qT[:, col:col + 1], None,
                                            ALU.mult).then_inc(ks_ready, 1)
            weight_high(0)

            def row_max(i):
                dve.wait_ge(score_ready, i + 1)
                nc.vector.reduce_max(negmax[:, i:i + 1], score_ps[i][:], AX_X, negate=True).then_inc(negmax_ready, 1)

            def half_pT(i):
                dve.wait_ge(pT_tp, i + 1)
                nc.vector.tensor_copy(pT[:, i, 256:512], pT_ps[i][1][:, 0:256]).then_inc(pT_dve, 1)

            def attended(i):
                dve.wait_ge(prob_ready, i + 1)
                then(nc.vector.reciprocal(probrec[:, i:i + 1], probsum[:, i:i + 1]))
                dve.wait_ge(attn_ready, i + 1)
                nc.vector.scalar_tensor_tensor(out=x1[:, i], in0=attn_ps[i][:, 0:D], scalar=probrec[:, i:i + 1],
                                               in1=xs[:, i], op0=ALU.mult, op1=ALU.add).then_inc(x1_ready, 1)
                dve.wait_ge(x1_ready, i + 1)
                row_stats(x1, i)

            def norm1(b):
                tiles = range(b * TB, (b + 1) * TB)
                aggregate(tiles)
                var = meanvar[:, b * TB:(b + 1) * TB, 1]
                nc.vector.tensor_scalar(var_eps[:, 0:TB], var, 1.0 + EPS, EPS * EPS, ALU.mult, ALU.add).then_inc(dve_step, 1)
                steps[0] += 1
                then(nc.vector.tensor_scalar(var_eps[:, TB:2 * TB], var, EPS, None, ALU.add))
                rsqrt(2 * TB)
                for k, i in enumerate(tiles):
                    normalized(u1, x1, i, k).then_inc(u1_ready, 1)
                for k, i in enumerate(tiles):
                    normalized(z, x1, i, TB + k).then_inc(z_ready, 1)

            def norm2(b):
                tiles = range(b * TB, (b + 1) * TB)
                for i in tiles:
                    dve.wait_ge(mix_ready, i + 1)
                    dve.wait_ge(zb_ready, i + 1)
                    nc.vector.tensor_tensor(x2[:, i], mix_ps[i][:, 0:D], zb[:, i], ALU.add).then_inc(x2_ready, 1)
                for i in tiles:
                    dve.wait_ge(x2_ready, i + 1)
                    row_stats(x2, i)
                aggregate(tiles)
                then(nc.vector.tensor_scalar(var_eps[:, 0:TB], meanvar[:, b * TB:(b + 1) * TB, 1], EPS, None, ALU.add))
                dve.wait_ge(z_ready, (b + 1) * TB)
                rsqrt(TB)
                for k, i in enumerate(tiles):
                    normalized(u2, x2, i, k).then_inc(u2_ready, 1)

            def split_n2(b):
                cols = slice(b * S, (b + 1) * S)
                dve.wait_ge(n2T_ready, b + 1)
                nc.vector.tensor_copy(n2h[:, cols], n2T[:, cols]).then_inc(n2h_ready, 1)
                dve.wait_ge(n2h_ready, b + 1)
                nc.vector.tensor_tensor(n2l[:, cols], n2T[:, cols], n2h[:, cols].bitcast(F32),
                                        ALU.subtract).then_inc(n2l_ready, 1)

            row_max(0)
            row_max(1)
            half_pT(0)
            row_max(2)
            half_pT(1)
            row_max(3)
            weight_high(1)
            attended(0)
            attended(1)
            half_pT(2)
            norm1(0)
            half_pT(3)
            attended(2)
            attended(3)
            norm1(1)
            norm2(0)
            split_n2(0)
            norm2(1)
            split_n2(1)

            dve.wait_ge(logit_ready, T)
            logits = logit_ps[:, 0:T * E].rearrange("p (t e) -> p t e", e=E)
            then(nc.vector.reduce_max(negtop[:], logits, AX_X, negate=True))
            nc.vector.tensor_tensor(lshift[:], logits, negtop[:].unsqueeze(2).broadcast_to([P, T, E]),
                                    ALU.add).then_inc(lshift_ready, 1)
            weight_high(2)
            dve.wait_ge(gate_ready, 1)
            then(nc.vector.reduce_sum(gate_sum[:], gate[:, :, 0:E], AX_X))
            then(nc.vector.reciprocal(gate_rec[:], gate_sum[:]))
            for i in range(T):
                then(nc.vector.max(top8[:, i], gate[:, i, 0:E]))
            then(nc.vector.tensor_copy(wanted[:, :, 0:TOP_K], top8[:, :, 0:TOP_K]))
            for i in range(T):
                then(nc.vector.match_replace(gate_rest[:, i], wanted[:, i], gate[:, i], 0.0))
            then(nc.vector.tensor_tensor(picked[:], gate[:, :, 0:E], gate_rest[:, :, 0:E], ALU.subtract))
            nc.vector.tensor_tensor(weight[:], picked[:], gate_rec[:].unsqueeze(2).broadcast_to([P, T, E]),
                                    ALU.mult).then_inc(weight_ready, 1)
            dve.wait_ge(weightT_tp, 1)
            nc.vector.tensor_copy(weightT[:], rowsT_ps[0:E, :]).then_inc(weightT_ready, 1)

            def low_part(n):
                dve.wait_ge(hidh_ready, n + 1)
                if n >= H_BUFS:
                    dve.wait_ge(hid_used, n - H_BUFS + 1)
                nc.vector.tensor_tensor(hidl[:, n % H_BUFS], hid[:, n % H_BUFS], hidh[:, n % H_BUFS].bitcast(F32),
                                        ALU.subtract).then_inc(hidl_ready, 1)

            def weigh(e):
                dve.wait_ge(hid_used, (e + 1) * FC)
                dve.wait_ge(spread_in[e], 16)
                if e >= 3:
                    dve.wait_ge(acc_ready, e - 1)
                nc.vector.tensor_tensor(y_part[:, e % 2], y_ps[e % 2][:], weight_all[:, e], ALU.mult).then_inc(y_part_ready, 1)
                if e == 0:
                    dve.wait_ge(y_part_ready, 1)
                    dve.wait_ge(b2_ready, 1)
                    nc.vector.tensor_tensor(acc[:], b2_ps[:], y_part[:, 0], ALU.add).then_inc(acc_ready, 1)
                if e == E - 1:
                    dve.wait_ge(y_part_ready, E)
                    dve.wait_ge(acc_ready, E - 1)
                    nc.vector.tensor_tensor(acc[:], acc[:], y_part[:, e % 2], ALU.add).then_inc(acc_ready, 1)

            for n in range(NCH):
                low_part(n)
                if n % FC == 1 and n // FC + 3 < E:
                    weight_high(n // FC + 3)
                if n >= FC + LAG and (n - FC - LAG) % FC == 0:
                    weigh((n - FC - LAG) // FC)
            weigh(E - 1)
            dve.wait_ge(resid_ready, T)
            for half in range(2):
                dve.wait_ge(acc_tp, half + 1)
                nc.vector.tensor_tensor(result[:, 2 * half:2 * half + 2].rearrange("p t d -> p (t d)"), outT_ps[half][:, 0:S],
                                        resid[:, 2 * half:2 * half + 2].rearrange("p t d -> p (t d)"),
                                        ALU.add).then_inc(result_ready, 1)

        @block.tensor
        def _(pe):
            pe.wait_ge(ident_ready, 1)
            pe.wait_ge(rows_in, 80)
            nc.tensor.transpose(const_ps[:, 0:ROWS], const_rows[:], ident[0:ROWS, 0:ROWS]).then_inc(const_tp, 1)
            for i in range(T):
                pe.wait_ge(qn_ready, i + 1)
                last = nc.tensor.transpose(qT_ps[i // TB][:, i % TB * P:(i % TB + 1) * P], qn[:, i], ident[:])
                if i % TB == TB - 1:
                    last.then_inc(qT_tp, 1)
            for b in range(B):
                for j in range(KC):
                    pe.wait_ge(ks_ready, b * KC + j + 1)
                    last = nc.tensor.transpose(kT_ps[b][:, j * P:(j + 1) * P], ks[:, b, j], ident[:])
                last.then_inc(kT_tp, 1)

            def scores(i):
                pe.wait_ge(qT_ready, i // TB + 1)
                pe.wait_ge(kT_ready, i // TB + 1)
                nc.tensor.matmul(score_ps[i][:], qT[:, i * P:(i + 1) * P], kT[:, i // TB], start=True,
                                 stop=True).then_inc(score_ready, 1)

            def turn_probs(i):
                pe.wait_ge(prob_ready, i + 1)
                if i == 0:
                    pe.wait_ge(qT_ready, B)
                    pe.wait_ge(const_ready, 1)
                if i == 1:
                    pe.wait_ge(kT_ready, B)
                for j in range(KC):
                    last = nc.tensor.transpose(pT_ps[i][j // 2][:, j % 2 * P:(j % 2 + 1) * P], probs[:, i, j * P:(j + 1) * P], ident[:])
                last.then_inc(pT_tp, 1)

            def attend(i):
                pe.wait_ge(pT_act, i + 1)
                pe.wait_ge(pT_dve, i + 1)
                for j in range(KC):
                    last = nc.tensor.matmul(attn_ps[i][:, 0:D], pT[:, i, j * P:(j + 1) * P], kv[:, i // TB, j],
                                            start=(j == 0), stop=(j == KC - 1))
                last.then_inc(attn_ready, 1)

            def mix(b):
                for i in range(b * TB, (b + 1) * TB):
                    pe.wait_ge(u1_ready, i + 1)
                    last = nc.tensor.transpose(n1T_ps[b][:, i % TB * P:(i % TB + 1) * P], u1[:, i], ident[:])
                last.then_inc(u1_tp, 1)
                pe.wait_ge(n1T_ready, b + 1)
                if b == 0:
                    pe.wait_ge(mixwi_ready, 1)
                for i in range(b * TB, (b + 1) * TB):
                    nc.tensor.matmul(mix_ps[i][:, 0:D], n1T[:, i * P:(i + 1) * P], mixwi[:], start=True,
                                     stop=True).then_inc(mix_ready, 1)

            def route(b):
                for i in range(b * TB, (b + 1) * TB):
                    pe.wait_ge(u2_ready, i + 1)
                    last = nc.tensor.transpose(n2T_ps[b][:, i % TB * P:(i % TB + 1) * P], u2[:, i], ident[:])
                last.then_inc(u2_tp, 1)
                pe.wait_ge(n2T_ready, b + 1)
                if b == 0:
                    pe.wait_ge(routw_in, 16)
                for i in range(b * TB, (b + 1) * TB):
                    nc.tensor.matmul(logit_ps[:, i * E:(i + 1) * E], n2T[:, i * P:(i + 1) * P], routw[:], start=True,
                                     stop=True).then_inc(logit_ready, 1)

            for i in range(T):
                scores(i)
                if i >= 2:
                    turn_probs(i - 2)
            turn_probs(2)
            attend(0)
            turn_probs(3)
            attend(1)
            attend(2)
            attend(3)
            mix(0)
            mix(1)
            route(0)
            route(1)

            def hidden(n):
                e, w = n // FC, slice((n % FC) * P, (n % FC + 1) * P)
                if n == 0:
                    pe.wait_ge(n2h_ready, B)
                    pe.wait_ge(n2l_ready, B)
                if n >= H_BANKS:
                    pe.wait_ge(hid_ready, n - H_BANKS + 1)
                if n % FC == 0:
                    pe.wait_ge(w1h_ready, e + 1)
                    pe.wait_ge(w1l_ready, e + 1)
                ps = hid_ps[n % H_BANKS][:]
                nc.tensor.matmul(ps, w1h[:, e, w], n2h[:], start=True, stop=False)
                nc.tensor.matmul(ps, w1h[:, e, w], n2l[:], start=False, stop=False)
                nc.tensor.matmul(ps, w1l[:, e, w], n2h[:], start=False, stop=True).then_inc(hid_mm, 1)

            def project(n):
                e, c, buf = n // FC, n % FC, n % H_BUFS
                if c == 0:
                    pe.wait_ge(w2h_ready, e + 1)
                    pe.wait_ge(w2l_ready, e + 1)
                    if e >= 2:
                        pe.wait_ge(y_part_ready, e - 1)
                pe.wait_ge(hidh_ready, n + 1)
                ps = y_ps[e % 2][:]
                nc.tensor.matmul(ps, w2h[:, e, c], hidh[:, buf], start=(c == 0), stop=False)
                nc.tensor.matmul(ps, w2l[:, e, c], hidh[:, buf], start=False, stop=False)
                pe.wait_ge(hidl_ready, n + 1)
                nc.tensor.matmul(ps, w2h[:, e, c], hidl[:, buf], start=False, stop=(c == FC - 1)).then_inc(hid_used, 1)

            def turn_weights():
                pe.wait_ge(weight_ready, 1)
                for i in range(T):
                    last = nc.tensor.transpose(rowsT_ps[0:E, i * P:(i + 1) * P], weight[:, i], ident[:])
                last.then_inc(weightT_tp, 1)

            def weighted_b2():
                pe.wait_ge(weightT_ready, 1)
                pe.wait_ge(b2_in, 16)
                nc.tensor.matmul(b2_ps[:], b2s[:], weightT[:], start=True, stop=True).then_inc(b2_ready, 1)

            for n in range(NCH + LAG):
                if n < NCH:
                    hidden(n)
                if n == 2:
                    turn_weights()
                if n >= LAG:
                    project(n - LAG)
                if n == LAG:
                    weighted_b2()
            pe.wait_ge(acc_ready, E)
            for i in range(T):
                last = nc.tensor.transpose(outT_ps[i // TB][:, i % TB * P:(i % TB + 1) * P], acc[:, i * P:(i + 1) * P], ident[:])
                if i % 2:
                    last.then_inc(acc_tp, 1)


_INS = ['x', 'ctx_1024', 'L0_ffn_g1', 'L0_ffn_be1', 'L0_ffn_mix_w', 'L0_ffn_mix_b', 'L0_ffn_g2', 'L0_ffn_be2',
        'L0_ffn_router_w', 'L0_ffn_w1', 'L0_ffn_b1', 'L0_ffn_w2', 'L0_ffn_b2']
_OUT = ((2, 256, 128), 'float32')


def kernel(**inputs):
    import numpy as _np
    import concourse.bacc as _bacc
    from concourse import mybir as _mybir
    from concourse.bass_utils import run_bass_kernel_spmd as _run

    nc = _bacc.Bacc("TRN2", target_bir_lowering=False, num_devices=1)
    arrays, args = {}, []
    for name in _INS:
        a = _np.ascontiguousarray(inputs[name])
        arrays[f"in_{name}_dram"] = a
        args.append(nc.dram_tensor(f"in_{name}_dram", a.shape, _mybir.dt.from_np(a.dtype), kind="ExternalInput").ap())
    args.append(nc.dram_tensor("out_dram", _OUT[0], _mybir.dt.from_np(_np.dtype(_OUT[1])), kind="ExternalOutput").ap())
    xattn_moe_kernel(nc, *args)
    r = _run(nc, [arrays], core_ids=[0])
    return r.results[0]["out_dram"]
```

```python
from contextlib import ExitStack

import concourse.bass as bass
from concourse import mybir

F32 = mybir.dt.float32
F32R = mybir.dt.float32r
BF16 = mybir.dt.bfloat16
I32 = mybir.dt.int32
ALU = mybir.AluOpType
ACT = mybir.ActivationFunctionType
AX_X = mybir.AxisListType.X

P = 128
EPS = 1e-5
TOP_K = 2
RSQRT_C = 0.9185584209116459
RSQRT_K = 0.27141074355784134 * (1 - 1.9e-7)
RSQRT_A1, RSQRT_A0 = -4.253164463819023, 5.291916161234017
RSQRT_B1, RSQRT_B0 = -0.9063260470190041, 1.713536060778617


def xattn_moe_kernel(nc: bass.Bass, x, ctx_kv, g1, be1, mix_w, mix_b, g2, be2, router_w, w1, b1, w2, b2, out):
    B, S, D = x.shape
    SK = ctx_kv.shape[1]
    E, _, F = w1.shape
    T = B * S // P
    TB = S // P
    KC = SK // P
    FC = F // P
    N = B * S
    Q_STEP = S // KC
    QR = B * KC
    assert D == P and KC == 4 and N == 512 and B == 2

    NCH = E * FC
    H_BANKS = 3
    H_BUFS = 4
    LAG = 3
    WARM_START = 10
    WARM_NORMS = 26
    ROWS = NCH + 4
    G1, BE1, G2, BE2 = (slice(NCH + i, NCH + i + 1) for i in range(4))

    x_tok = x.rearrange("b (n p) d -> p (b n) d", p=P)
    x_scale_rows = x.rearrange("b (j s) d -> (b j) s d", s=Q_STEP)[:, 0, :]
    out_tok = out.rearrange("b (n p) d -> p (b n) d", p=P)
    kv_tok = ctx_kv.rearrange("b (n p) d -> b p n d", p=P)
    w1_view = w1.rearrange("e d f -> d e f")
    w2_view = w2.rearrange("e (c p) d -> p e c d", p=P)
    weight_rows = nc.dram_tensor("weight_rows", [E, N], F32, kind="Internal").ap()

    with ExitStack() as stack:
        def sb(name, shape, dt=F32):
            return stack.enter_context(nc.sbuf_tensor(name, shape, dt))

        def sem(name):
            return stack.enter_context(nc.semaphore(name))

        bank = [stack.enter_context(nc.psum_tensor(f"bank{i}", [P, 512], F32)) for i in range(8)]
        kT_ps, prep_ps, scale_ps, qT_ps = [bank[3], bank[4]], bank[0], [bank[1], bank[2]], [bank[5], bank[6]]
        score_ps = [bank[7], bank[3], bank[4], bank[5]]
        pT_ps = [(bank[1], bank[2]), (bank[6], bank[7]), (bank[3], bank[1]), (bank[4], bank[5])]
        attn_ps = [bank[2], bank[6], bank[3], bank[4]]
        x1T_ps, mix_ps = [bank[7], bank[1], bank[5], bank[2]], bank[0]
        n2T_ps, logit_ps = [bank[6], bank[3]], bank[4]
        hid_ps, y_ps = [bank[5], bank[7], bank[1]], [bank[0], bank[2]]
        weightT_ps, b2_ps = bank[6], bank[3]
        last_y_ps, accT_ps, last_yT_ps = [bank[2], bank[3]], [bank[4], bank[6]], [bank[0], bank[5]]

        warm_ps = bank[7]

        ident = sb("ident", [P, P])
        centering = sb("centering", [P, P])
        row_select = sb("row_select", [QR, QR, P])
        xs = sb("xs", [P, T, D])
        xrows = sb("xrows", [QR, D])
        kv = sb("kv", [P, B, KC, D])
        const_rows = sb("const_rows", [ROWS, P])
        const_cols = sb("const_cols", [P, ROWS])
        mixw = sb("mixw", [P, D])
        mixw1 = sb("mixw1", [P, D])
        mixwg = sb("mixwg", [P, D])
        mixwc = sb("mixwc", [P, D])
        be1_wide = sb("be1_wide", [P, P])
        mixb = sb("mixb", [P, D])
        be1_mixed = sb("be1_mixed", [P, D])
        mix_const = sb("mix_const", [P, D])
        routw = sb("routw", [P, E])
        b2s = sb("b2s", [E, D])
        w1s = sb("w1s", [P, E, F])
        w2s = sb("w2s", [P, E, FC, D])
        w1h = sb("w1h", [P, E, F], F32R)
        w1l = sb("w1l", [P, E, F], F32R)
        w2h = sb("w2h", [P, E, FC, D], F32R)
        w2l = sb("w2l", [P, E, FC, D], F32R)

        stats = sb("stats", [P, T + 1, 6])
        meanvar = sb("meanvar", [P, T + 1, 2])
        var_eps = sb("var_eps", [P, 2 * T])
        guess = sb("guess", [P, 2 * T])
        guess_k = sb("guess_k", [P, 2 * T])
        square = sb("square", [P, 2 * T])
        ratio = sb("ratio", [P, 2 * T])
        quad_a = sb("quad_a", [P, 2 * T])
        quad_b = sb("quad_b", [P, 2 * T])
        rstd0 = sb("rstd0", [P, T + 1])
        rstd1 = sb("rstd1", [P, 2 * T])
        rstd2 = sb("rstd2", [P, T])
        xc = sb("xc", [P, T, D])
        qn = sb("qn", [P, T, D])
        qrows = sb("qrows", [QR, D])
        qT = sb("qT", [P, N])
        kT = sb("kT", [P, B, SK])
        kTs = sb("kTs", [P, B, SK])
        negmax = sb("negmax", [P, T])
        probs = sb("probs", [P, T, SK])
        probsum = sb("probsum", [P, T])
        probrec = sb("probrec", [P, T])
        pT = sb("pT", [P, T, SK])
        x1 = sb("x1", [P, T, D])
        x1T = sb("x1T", [P, T, P])
        x1c = sb("x1c", [P, T, D])
        z = sb("z", [P, T, D])
        zb = sb("zb", [P, T, D])
        x2 = sb("x2", [P, T, D])
        x2c, u2 = xc, qn
        resid = sb("resid", [P, T, D])
        resid_acc = sb("resid_acc", [P, T, D])
        n2T = sb("n2T", [P, N])
        n2h = sb("n2h", [P, N], F32R)
        n2l = sb("n2l", [P, N], F32R)

        negtop = sb("negtop", [P, T])
        lshift = sb("lshift", [P, T, E])
        gate = sb("gate", [P, T, 2 * E])
        gate_rest = sb("gate_rest", [P, T, 2 * E])
        gate_sum = sb("gate_sum", [P, T])
        gate_rec = sb("gate_rec", [P, T])
        top8 = sb("top8", [P, T, 8])
        wanted = sb("wanted", [P, T, 8])
        picked = sb("picked", [P, T, E])
        weight = sb("weight", [P, T, E])
        weightT = sb("weightT", [E, N])
        weight_all = sb("weight_all", [P, E, N])

        hid, y_part, acc = probs, pT[:, 0:2], pT[:, 2]
        hidh = sb("hidh", [P, H_BUFS, N], F32R)
        hidl = sb("hidl", [P, H_BUFS, N], F32R)
        result = sb("result", [P, T, D])
        warm = sb("warm", [P, 1])
        zeros = sb("zeros", [P, 512], BF16)

        xrows_in, x_in, kv_in = sem("xrows_in"), [sem(f"x_in{b}") for b in range(B)], [sem(f"kv_in{b}") for b in range(B)]
        rows_in, mixw_in, mixb_in, routw_in, b2_in = (sem(n) for n in ("rows_in", "mixw_in", "mixb_in", "routw_in", "b2_in"))
        w1_in = [sem(f"w1_in{e}") for e in range(E)]
        w2_in = [sem(f"w2_in{e}") for e in range(E)]
        pool_step, ident_ready, center_ready, select_ready, mixw1_ready, mix_const_ready, warm_set = (
            sem(n) for n in ("pool_step", "ident_ready", "center_ready", "select_ready", "mixw1_ready", "mix_const_ready", "warm_set"))
        const_tp, const_ready, mixwg_ready, be1_ready, prep_mm, mixwc_ready, be1_mixed_ready = (
            sem(n) for n in ("const_tp", "const_ready", "mixwg_ready", "be1_ready", "prep_mm", "mixwc_ready", "be1_mixed_ready"))
        dve_step, zeros_ready = sem("dve_step"), sem("zeros_ready")
        kT_tp, kT_ready, rstd0_ready, xc_ready, qrows_ready, scale_mm, kTs_ready, qn_dve, qn_act, qT_tp, qT_ready = (
            sem(n) for n in ("kT_tp", "kT_ready", "rstd0_ready", "xc_ready", "qrows_ready", "scale_mm", "kTs_ready", "qn_dve",
                             "qn_act", "qT_tp", "qT_ready"))
        score_ready, negmax_ready, prob_ready, pT_tp, pT_act, pT_dve, attn_ready, x1_ready = (
            sem(n) for n in ("score_ready", "negmax_ready", "prob_ready", "pT_tp", "pT_act", "pT_dve", "attn_ready", "x1_ready"))
        x1T_tp, x1T_ready, mix_ready, x1c_ready, rstd1_ready, z_ready, zb_ready, zb_dve, x2_ready = (
            sem(n) for n in ("x1T_tp", "x1T_ready", "mix_ready", "x1c_ready", "rstd1_ready", "z_ready", "zb_ready", "zb_dve", "x2_ready"))
        x2c_ready, rstd2_ready, u2_dve, u2_act, u2_tp, n2T_ready, n2h_ready, n2l_ready, resid_ready = (
            sem(n) for n in ("x2c_ready", "rstd2_ready", "u2_dve", "u2_act", "u2_tp", "n2T_ready", "n2h_ready", "n2l_ready", "resid_ready"))
        logit_ready, lshift_ready, gate_ready, pads_ready, weight_ready, weightT_tp, weightT_ready = (
            sem(n) for n in ("logit_ready", "lshift_ready", "gate_ready", "pads_ready", "weight_ready", "weightT_tp", "weightT_ready"))
        weights_out, spread_in, b2_ready = sem("weights_out"), [sem(f"spread_in{e}") for e in range(E)], sem("b2_ready")
        w1h_ready, w2h_ready, w1l_ready, w2l_ready = (sem(n) for n in ("w1h_ready", "w2h_ready", "w1l_ready", "w2l_ready"))
        hid_mm, hid_ready, hidh_ready, hidl_ready, hid_used, y_part_ready, acc_ready = (
            sem(n) for n in ("hid_mm", "hid_ready", "hidh_ready", "hidl_ready", "hid_used", "y_part_ready", "acc_ready"))
        last_y_ready, last_part_ready, acc_tp, resid_acc_ready, last_yT_tp, result_ready, out_done = (
            sem(n) for n in ("last_y_ready", "last_part_ready", "acc_tp", "resid_acc_ready", "last_yT_tp", "result_ready", "out_done"))

        block = stack.enter_context(nc.Block())

        def tok(b):
            return slice(b * S, (b + 1) * S)

        def flat(tile, b):
            return tile[:, b * TB:(b + 1) * TB].rearrange("p t d -> p (t d)")

        @block.sync
        def _(sp):
            sp.dma_start(xrows[:], x_scale_rows).then_inc(xrows_in, 16)
            for b in range(B):
                sp.dma_start(xs[:, b * TB:(b + 1) * TB], x_tok[:, b * TB:(b + 1) * TB]).then_inc(x_in[b], 16)
            for b in range(B):
                sp.dma_start(kv[:, b], kv_tok[b]).then_inc(kv_in[b], 16)
            sp.dma_start(const_rows[0:NCH, :], b1.rearrange("e (c p) -> (e c) p", p=P)).then_inc(rows_in, 16)
            for i, v in enumerate((g1, be1, g2, be2)):
                sp.dma_start(const_rows[NCH + i:NCH + i + 1, :], v.rearrange("(o d) -> o d", o=1)).then_inc(rows_in, 16)
            sp.dma_start(mixw[:], mix_w).then_inc(mixw_in, 16)
            for e in range(E):
                sp.dma_start(w1s[:, e], w1_view[:, e]).then_inc(w1_in[e], 16)
                sp.dma_start(w2s[:, e], w2_view[:, e]).then_inc(w2_in[e], 16)
                if e == 0:
                    sp.dma_start(mixb[:], mix_b.partition_broadcast(P)).then_inc(mixb_in, 16)
                    sp.dma_start(routw[:], router_w).then_inc(routw_in, 16)
                    sp.dma_start(b2s[:], b2).then_inc(b2_in, 16)
            sp.wait_ge(weightT_ready, 1)
            sp.dma_start(weight_rows, weightT[:]).then_inc(weights_out, 16)
            sp.wait_ge(weights_out, 16)
            for e in range(E):
                sp.dma_start(weight_all[:, e, :], weight_rows[e, :].partition_broadcast(P)).then_inc(spread_in[e], 16)
            for half in range(2):
                sp.wait_ge(result_ready, half + 1)
                sp.dma_start(out_tok[:, half * TB:(half + 1) * TB], result[:, half * TB:(half + 1) * TB]).then_inc(out_done, 16)
            sp.wait_ge(out_done, 32)

        @block.gpsimd
        def _(pool):
            nc.gpsimd.memset(ident[:], 0.0).then_inc(pool_step, 1)
            pool.wait_ge(pool_step, 1)
            nc.gpsimd.affine_select(out=ident[:], in_=ident[:], compare_op=ALU.not_equal, fill=1.0, base=0,
                                    pattern=[[-1, P]], channel_multiplier=1).then_inc(ident_ready, 1)
            nc.gpsimd.memset(row_select[:], 0.0).then_inc(pool_step, 1)
            pool.wait_ge(pool_step, 2)
            nc.gpsimd.affine_select(out=row_select[:], in_=row_select[:], compare_op=ALU.not_equal, fill=1.0, base=0,
                                    pattern=[[-1, QR], [0, P]], channel_multiplier=1).then_inc(select_ready, 1)
            pool.wait_ge(ident_ready, 1)
            nc.gpsimd.tensor_scalar(centering[:], ident[:], -1.0 / D, None, ALU.add).then_inc(center_ready, 1)
            pool.wait_ge(mixw_in, 16)
            nc.gpsimd.tensor_tensor(mixw1[:], mixw[:], ident[:], ALU.add).then_inc(mixw1_ready, 1)

            def low_parts(e):
                pool.wait_ge(w1h_ready, e + 1)
                nc.gpsimd.tensor_tensor(w1l[:, e], w1s[:, e], w1h[:, e].bitcast(F32), ALU.subtract).then_inc(w1l_ready, 1)
                pool.wait_ge(w2h_ready, e + 1)
                nc.gpsimd.tensor_tensor(w2l[:, e], w2s[:, e], w2h[:, e].bitcast(F32), ALU.subtract).then_inc(w2l_ready, 1)

            low_parts(0)
            pool.wait_ge(mixb_in, 16)
            pool.wait_ge(be1_mixed_ready, 1)
            nc.gpsimd.tensor_tensor(mix_const[:], be1_mixed[:], mixb[:], ALU.add).then_inc(mix_const_ready, 1)
            low_parts(1)
            low_parts(2)
            pool.wait_ge(mix_const_ready, 1)
            for i in range(TB, T):
                pool.wait_ge(z_ready, i - TB + 1)
                nc.gpsimd.tensor_tensor(zb[:, i], z[:, i], mix_const[:], ALU.add).then_inc(zb_ready, 1)
            for i in range(T):
                pool.wait_ge(x2_ready, i + 1)
                nc.gpsimd.tensor_tensor(resid[:, i], x1[:, i], x2[:, i], ALU.add).then_inc(resid_ready, 1)
            low_parts(3)
            for e in range(E - 2):
                if e + 4 < E:
                    low_parts(e + 4)
                if e:
                    pool.wait_ge(y_part_ready, e + 1)
                    pool.wait_ge(acc_ready, e)
                    nc.gpsimd.tensor_tensor(acc, acc, y_part[:, e % 2], ALU.add).then_inc(acc_ready, 1)

        @block.scalar
        def _(act):
            act.wait_ge(warm_set, 1)
            nc.scalar.activation(warm[:], warm[:], ACT.Exp)

            def keys_turned(b):
                act.wait_ge(kT_tp, b + 1)
                nc.scalar.copy(kT[:, b], kT_ps[b][:]).then_inc(kT_ready, 1)

            keys_turned(0)
            act.wait_ge(rstd0_ready, 1)
            act.wait_ge(xc_ready, T)
            for i in range(TB, T):
                nc.scalar.activation(qn[:, i], xc[:, i], ACT.Copy, scale=rstd0[:, i:i + 1]).then_inc(qn_act, 1)
            for b in range(B):
                act.wait_ge(qT_tp, b + 1)
                nc.scalar.copy(qT[:, tok(b)], qT_ps[b][:, 0:S]).then_inc(qT_ready, 1)
                if b == 0:
                    keys_turned(1)
            act.wait_ge(const_tp, 1)
            nc.scalar.copy(const_cols[:], prep_ps[:, 0:ROWS]).then_inc(const_ready, 1)
            act.wait_ge(const_ready, 1)
            act.wait_ge(mixw1_ready, 1)
            nc.scalar.activation(mixwg[:], mixw1[:], ACT.Copy, scale=const_cols[:, G1]).then_inc(mixwg_ready, 1)
            nc.scalar.activation(be1_wide[:], ident[:], ACT.Identity, bias=const_cols[:, BE1], scale=0.0).then_inc(be1_ready, 1)

            def softmax(i):
                act.wait_ge(negmax_ready, i + 1)
                nc.scalar.activation(probs[:, i], score_ps[i][:], ACT.Exp, bias=negmax[:, i:i + 1],
                                     accum_out=probsum[:, i:i + 1]).then_inc(prob_ready, 1)

            def half_pT(i):
                act.wait_ge(pT_tp, i + 1)
                nc.scalar.copy(pT[:, i, 0:256], pT_ps[i][0][:, 0:256]).then_inc(pT_act, 1)

            def x1_turned(i):
                act.wait_ge(x1T_tp, i + 1)
                nc.scalar.copy(x1T[:, i], x1T_ps[i][:, 0:P]).then_inc(x1T_ready, 1)

            softmax(0)
            softmax(1)
            half_pT(0)
            act.wait_ge(prep_mm, 1)
            nc.scalar.copy(mixwc[:], prep_ps[:, 0:D]).then_inc(mixwc_ready, 1)
            nc.scalar.copy(be1_mixed[:], prep_ps[:, D:2 * D]).then_inc(be1_mixed_ready, 1)
            softmax(2)
            half_pT(1)
            softmax(3)
            half_pT(2)
            x1_turned(0)
            half_pT(3)
            for i in range(1, T):
                x1_turned(i)
            act.wait_ge(rstd1_ready, 1)
            act.wait_ge(x1c_ready, T)
            for i in range(TB, T):
                nc.scalar.activation(z[:, i], x1c[:, i], ACT.Copy, scale=rstd1[:, T + i:T + i + 1]).then_inc(z_ready, 1)
            act.wait_ge(rstd2_ready, 1)
            act.wait_ge(x2c_ready, T)
            for i in range(TB, T):
                nc.scalar.activation(u2[:, i], x2c[:, i], ACT.Copy, scale=rstd2[:, i:i + 1]).then_inc(u2_act, 1)
            for b in range(B):
                act.wait_ge(u2_tp, b + 1)
                nc.scalar.activation(n2T[:, tok(b)], n2T_ps[b][:, 0:S], ACT.Identity, bias=const_cols[:, BE2],
                                     scale=const_cols[:, G2]).then_inc(n2T_ready, 1)
            act.wait_ge(lshift_ready, 1)
            act.wait_ge(pads_ready, 1)
            nc.scalar.activation(gate[:, :, 0:E], lshift[:], ACT.Exp).then_inc(gate_ready, 1)

            def silu(n):
                act.wait_ge(hid_mm, n + 1)
                if n >= H_BUFS:
                    act.wait_ge(hidl_ready, n - H_BUFS + 1)
                nc.scalar.activation(hid[:, n % H_BUFS], hid_ps[n % H_BANKS][:], ACT.Silu,
                                     bias=const_cols[:, n:n + 1]).then_inc(hid_ready, 1)

            def high_part(n):
                act.wait_ge(hid_ready, n + 1)
                if n >= H_BUFS:
                    act.wait_ge(hid_used, n - H_BUFS + 1)
                nc.scalar.copy(hidh[:, n % H_BUFS], hid[:, n % H_BUFS]).then_inc(hidh_ready, 1)

            for n in range(NCH - 1):
                silu(n)
                if n:
                    high_part(n - 1)
            n = NCH - 1
            buf = n % H_BUFS
            act.wait_ge(hidl_ready, n - H_BUFS + 1)
            for half in range(2):
                act.wait_ge(hid_mm, n + half + 1)
                nc.scalar.activation(hid[:, buf, tok(half)], hid_ps[(n + half) % H_BANKS][:, 0:S], ACT.Silu,
                                     bias=const_cols[:, n:n + 1]).then_inc(hid_ready, 1)
                if half == 0:
                    high_part(n - 1)
                    act.wait_ge(hid_used, n - H_BUFS + 1)
                act.wait_ge(hid_ready, n + half + 1)
                nc.scalar.copy(hidh[:, buf, tok(half)], hid[:, buf, tok(half)]).then_inc(hidh_ready, 1)

        @block.vector
        def _(dve):
            steps = [0]

            def step(ins):
                steps[0] += 1
                ins.then_inc(dve_step, 1)

            def settle():
                dve.wait_ge(dve_step, steps[0])

            def rsqrt(y, done, fillers):
                n = y.shape[1]
                v, g, gk, sq, r = var_eps[:, 0:n], guess[:, 0:n], guess_k[:, 0:n], square[:, 0:n], ratio[:, 0:n]
                qa, qb = quad_a[:, 0:n], quad_b[:, 0:n]
                fillers = list(fillers)

                def fill(count):
                    for _ in range(min(count, len(fillers))):
                        fillers.pop(0)()

                step(nc.vector.tensor_scalar(g.bitcast(I32), v.bitcast(I32), 1, 0x7FFFFFFF, ALU.logical_shift_right,
                                             ALU.bitwise_xor))
                fill(1)
                settle()
                step(nc.vector.scalar_tensor_tensor(out=sq, in0=g, scalar=2.0 ** -66, in1=g, op0=ALU.mult, op1=ALU.mult))
                step(nc.vector.tensor_scalar(gk, g, RSQRT_K * RSQRT_C ** 0.5 * 2.0 ** -65.5, None, ALU.mult))
                fill(1)
                settle()
                step(nc.vector.scalar_tensor_tensor(out=r, in0=sq, scalar=RSQRT_C * 2.0 ** -65, in1=v, op0=ALU.mult,
                                                    op1=ALU.mult))
                fill(1)
                settle()
                step(nc.vector.scalar_tensor_tensor(out=qb, in0=r, scalar=RSQRT_B1, in1=r, op0=ALU.add, op1=ALU.mult))
                step(nc.vector.scalar_tensor_tensor(out=qa, in0=r, scalar=RSQRT_A1, in1=r, op0=ALU.add, op1=ALU.mult))
                fill(1)
                settle()
                step(nc.vector.scalar_tensor_tensor(out=qb, in0=qb, scalar=RSQRT_B0, in1=gk, op0=ALU.add, op1=ALU.mult))
                fill(len(fillers))
                settle()
                nc.vector.scalar_tensor_tensor(out=y, in0=qa, scalar=RSQRT_A0, in1=qb, op0=ALU.add,
                                               op1=ALU.mult).then_inc(done, 1)
                dve.wait_ge(done, 1)

            def centered(dst, src, done):
                return [lambda i=i: nc.vector.tensor_scalar(dst[:, i], src[:, i], meanvar[:, i, 0:1], None,
                                                            ALU.subtract).then_inc(done, 1) for i in range(T)]

            def weight_high(e):
                dve.wait_ge(w1_in[e], 16)
                nc.vector.tensor_copy(w1h[:, e], w1s[:, e]).then_inc(w1h_ready, 1)
                dve.wait_ge(w2_in[e], 16)
                nc.vector.tensor_copy(w2h[:, e], w2s[:, e]).then_inc(w2h_ready, 1)

            nc.vector.memset(zeros[:], 0.0).then_inc(zeros_ready, 1)
            nc.vector.memset(warm[:], 0.0).then_inc(warm_set, 1)
            nc.vector.memset(gate[:], -1.0).then_inc(pads_ready, 1)
            step(nc.vector.memset(wanted[:], -1.0))
            step(nc.vector.memset(meanvar[:], 1.0))

            dve.wait_ge(xrows_in, 16)
            step(nc.vector.bn_stats(stats[0:QR, T], xrows[:]))
            for i in range(T):
                dve.wait_ge(x_in[i // TB], 16)
                step(nc.vector.bn_stats(stats[:, i], xs[:, i]))
            settle()
            step(nc.vector.bn_aggr(meanvar[0:QR, T], stats[0:QR, T]))
            for i in range(T):
                step(nc.vector.bn_aggr(meanvar[:, i], stats[:, i]))
            settle()
            step(nc.vector.tensor_scalar(var_eps[:, 0:T + 1], meanvar[:, :, 1], EPS, None, ALU.add))
            settle()
            rsqrt(rstd0[:], rstd0_ready, centered(xc, xs, xc_ready))
            nc.vector.tensor_scalar(qrows[:], xrows[:], meanvar[0:QR, T, 0:1], rstd0[0:QR, T:T + 1], ALU.subtract,
                                    ALU.mult).then_inc(qrows_ready, 1)
            dve.wait_ge(xc_ready, T)
            for i in range(TB):
                nc.vector.tensor_scalar(qn[:, i], xc[:, i], rstd0[:, i:i + 1], None, ALU.mult).then_inc(qn_dve, 1)
            for b in range(B):
                dve.wait_ge(kT_ready, b + 1)
                dve.wait_ge(scale_mm, b + 1)
                nc.vector.tensor_tensor(kTs[:, b], kT[:, b], scale_ps[b][:], ALU.mult).then_inc(kTs_ready, 1)
            weight_high(0)

            def row_max(i):
                dve.wait_ge(score_ready, i + 1)
                nc.vector.reduce_max(negmax[:, i:i + 1], score_ps[i][:], AX_X, negate=True).then_inc(negmax_ready, 1)

            def half_pT(i):
                dve.wait_ge(pT_tp, i + 1)
                nc.vector.tensor_copy(pT[:, i, 256:512], pT_ps[i][1][:, 0:256]).then_inc(pT_dve, 1)

            def recip_sum(i):
                dve.wait_ge(prob_ready, i + 1)
                step(nc.vector.reciprocal(probrec[:, i:i + 1], probsum[:, i:i + 1]))

            def attended(i):
                settle()
                dve.wait_ge(attn_ready, i + 1)
                nc.vector.scalar_tensor_tensor(out=x1[:, i], in0=attn_ps[i][:, 0:D], scalar=probrec[:, i:i + 1],
                                               in1=xs[:, i], op0=ALU.mult, op1=ALU.add).then_inc(x1_ready, 1)

            def x1_stats(i):
                dve.wait_ge(x1_ready, i + 1)
                step(nc.vector.bn_stats(stats[:, i], x1[:, i]))

            row_max(0)
            row_max(1)
            weight_high(1)
            weight_high(2)
            half_pT(0)
            recip_sum(0)
            row_max(2)
            half_pT(1)
            recip_sum(1)
            attended(0)
            row_max(3)
            half_pT(2)
            recip_sum(2)
            attended(1)
            x1_stats(0)
            half_pT(3)
            recip_sum(3)
            x1_stats(1)
            attended(2)
            x1_stats(2)
            attended(3)
            x1_stats(3)

            settle()
            for i in range(T):
                step(nc.vector.bn_aggr(meanvar[:, i], stats[:, i]))
            settle()
            step(nc.vector.tensor_scalar(var_eps[:, 0:T], meanvar[:, 0:T, 1], 1.0 + EPS, EPS * EPS, ALU.mult, ALU.add))
            step(nc.vector.tensor_scalar(var_eps[:, T:2 * T], meanvar[:, 0:T, 1], EPS, None, ALU.add))
            settle()
            rsqrt(rstd1[:], rstd1_ready, centered(x1c, x1, x1c_ready))
            dve.wait_ge(x1c_ready, T)
            dve.wait_ge(mix_const_ready, 1)
            for i in range(TB):
                nc.vector.scalar_tensor_tensor(out=zb[:, i], in0=x1c[:, i], scalar=rstd1[:, T + i:T + i + 1],
                                               in1=mix_const[:], op0=ALU.mult, op1=ALU.add).then_inc(zb_dve, 1)
            dve.wait_ge(mix_ready, T)
            for i in range(T):
                if i < TB:
                    dve.wait_ge(zb_dve, i + 1)
                else:
                    dve.wait_ge(zb_ready, i - TB + 1)
                nc.vector.scalar_tensor_tensor(out=x2[:, i], in0=mix_ps[:, i * D:(i + 1) * D], scalar=rstd1[:, i:i + 1],
                                               in1=zb[:, i], op0=ALU.mult, op1=ALU.add).then_inc(x2_ready, 1)
                if i:
                    dve.wait_ge(x2_ready, i)
                    step(nc.vector.bn_stats(stats[:, i - 1], x2[:, i - 1]))
            dve.wait_ge(x2_ready, T)
            step(nc.vector.bn_stats(stats[:, T - 1], x2[:, T - 1]))
            settle()
            for i in range(T):
                step(nc.vector.bn_aggr(meanvar[:, i], stats[:, i]))
            settle()
            step(nc.vector.tensor_scalar(var_eps[:, 0:T], meanvar[:, 0:T, 1], EPS, None, ALU.add))
            settle()
            rsqrt(rstd2[:], rstd2_ready, centered(x2c, x2, x2c_ready))
            dve.wait_ge(x2c_ready, T)
            for i in range(TB):
                nc.vector.tensor_scalar(u2[:, i], x2c[:, i], rstd2[:, i:i + 1], None, ALU.mult).then_inc(u2_dve, 1)
            for b in range(B):
                dve.wait_ge(n2T_ready, b + 1)
                nc.vector.tensor_copy(n2h[:, tok(b)], n2T[:, tok(b)]).then_inc(n2h_ready, 1)
                dve.wait_ge(n2h_ready, b + 1)
                nc.vector.tensor_tensor(n2l[:, tok(b)], n2T[:, tok(b)], n2h[:, tok(b)].bitcast(F32),
                                        ALU.subtract).then_inc(n2l_ready, 1)

            dve.wait_ge(logit_ready, T)
            logits = logit_ps[:, 0:T * E].rearrange("p (t e) -> p t e", e=E)
            step(nc.vector.reduce_max(negtop[:], logits, AX_X, negate=True))
            settle()
            nc.vector.tensor_tensor(lshift[:], logits, negtop[:].unsqueeze(2).broadcast_to([P, T, E]),
                                    ALU.add).then_inc(lshift_ready, 1)
            weight_high(3)

            def route_sums():
                dve.wait_ge(gate_ready, 1)
                step(nc.vector.reduce_sum(gate_sum[:], gate[:, :, 0:E], AX_X))
                for i in range(T):
                    step(nc.vector.max(top8[:, i], gate[:, i, 0:E]))
                settle()
                step(nc.vector.reciprocal(gate_rec[:], gate_sum[:]))
                step(nc.vector.tensor_copy(wanted[:, :, 0:TOP_K], top8[:, :, 0:TOP_K]))

            def route_pick():
                settle()
                for i in range(T):
                    step(nc.vector.match_replace(gate_rest[:, i], wanted[:, i], gate[:, i], 0.0))
                settle()
                step(nc.vector.tensor_tensor(picked[:], gate[:, :, 0:E], gate_rest[:, :, 0:E], ALU.subtract))

            def route_weights():
                settle()
                nc.vector.tensor_tensor(weight[:], picked[:], gate_rec[:].unsqueeze(2).broadcast_to([P, T, E]),
                                        ALU.mult).then_inc(weight_ready, 1)

            def route_turned():
                dve.wait_ge(weightT_tp, 1)
                nc.vector.tensor_copy(weightT[:], weightT_ps[0:E, :]).then_inc(weightT_ready, 1)

            def low_part(n):
                dve.wait_ge(hidh_ready, n + 1)
                if n >= H_BUFS:
                    dve.wait_ge(hid_used, n - H_BUFS + 1)
                nc.vector.tensor_tensor(hidl[:, n % H_BUFS], hid[:, n % H_BUFS], hidh[:, n % H_BUFS].bitcast(F32),
                                        ALU.subtract).then_inc(hidl_ready, 1)

            def weigh(e):
                dve.wait_ge(hid_used, (e + 1) * FC)
                dve.wait_ge(spread_in[e], 16)
                if e >= 3:
                    dve.wait_ge(acc_ready, e - 1)
                nc.vector.tensor_tensor(y_part[:, e % 2], y_ps[e % 2][:], weight_all[:, e], ALU.mult).then_inc(y_part_ready, 1)
                if e == 0:
                    dve.wait_ge(b2_ready, 1)
                    dve.wait_ge(y_part_ready, 1)
                    nc.vector.tensor_tensor(acc, b2_ps[:], y_part[:, 0], ALU.add).then_inc(acc_ready, 1)
                if e == E - 2:
                    dve.wait_ge(acc_ready, e)
                    dve.wait_ge(y_part_ready, e + 1)
                    nc.vector.tensor_tensor(acc, acc, y_part[:, e % 2], ALU.add).then_inc(acc_ready, 1)

            routing = {0: route_sums, 1: route_pick, 2: route_weights, 5: route_turned}
            for n in range(NCH - 1):
                low_part(n)
                if n in routing:
                    routing[n]()
                if n % FC == 1 and n // FC + 4 < E:
                    weight_high(n // FC + 4)
                if n >= 2 * FC and n % FC == 0:
                    weigh(n // FC - 2)
            weigh(E - 2)
            n = NCH - 1
            buf = n % H_BUFS
            dve.wait_ge(hid_used, n - H_BUFS + 1)
            for half in range(2):
                dve.wait_ge(hidh_ready, n + half + 1)
                nc.vector.tensor_tensor(hidl[:, buf, tok(half)], hid[:, buf, tok(half)], hidh[:, buf, tok(half)].bitcast(F32),
                                        ALU.subtract).then_inc(hidl_ready, 1)
            dve.wait_ge(resid_ready, T)
            dve.wait_ge(acc_tp, 1)
            for half in range(2):
                nc.vector.tensor_tensor(flat(resid_acc, half), accT_ps[half][:, 0:S], flat(resid, half),
                                        ALU.add).then_inc(resid_acc_ready, 1)
            dve.wait_ge(spread_in[E - 1], 16)
            for half in range(2):
                dve.wait_ge(last_y_ready, half + 1)
                nc.vector.tensor_tensor(y_part[:, (E - 1) % 2, tok(half)], last_y_ps[half][:, 0:S],
                                        weight_all[:, E - 1, tok(half)], ALU.mult).then_inc(last_part_ready, 1)
            for half in range(2):
                dve.wait_ge(resid_acc_ready, half + 1)
                dve.wait_ge(last_yT_tp, half + 1)
                nc.vector.tensor_tensor(flat(result, half), last_yT_ps[half][:, 0:S], flat(resid_acc, half),
                                        ALU.add).then_inc(result_ready, 1)

        @block.tensor
        def _(pe):
            def keep_warm(products):
                for _ in range(products):
                    nc.tensor.matmul(warm_ps[:], zeros[:, 0:P], zeros[:], start=True, stop=True)

            def turn(dst, n, src):
                return nc.tensor.transpose(dst[:, n * P:(n + 1) * P], src, ident[:])

            pe.wait_ge(zeros_ready, 1)
            keep_warm(WARM_START)
            pe.wait_ge(ident_ready, 1)
            for b in range(B):
                pe.wait_ge(kv_in[b], 16)
                for j in range(KC):
                    last = turn(kT_ps[b], j, kv[:, b, j])
                last.then_inc(kT_tp, 1)
            pe.wait_ge(qrows_ready, 1)
            pe.wait_ge(select_ready, 1)
            for b in range(B):
                for j in range(KC):
                    last = nc.tensor.matmul(scale_ps[b][:, j * P:(j + 1) * P], row_select[:, b * KC + j], qrows[:],
                                            start=True, stop=True)
                last.then_inc(scale_mm, 1)
                for k in range(TB):
                    if b == 0:
                        pe.wait_ge(qn_dve, k + 1)
                    else:
                        pe.wait_ge(qn_act, k + 1)
                    last = turn(qT_ps[b], k, qn[:, b * TB + k])
                last.then_inc(qT_tp, 1)
            pe.wait_ge(rows_in, 80)
            nc.tensor.transpose(prep_ps[:, 0:ROWS], const_rows[:], ident[0:ROWS, 0:ROWS]).then_inc(const_tp, 1)

            def scores(i):
                pe.wait_ge(qT_ready, i // TB + 1)
                pe.wait_ge(kTs_ready, i // TB + 1)
                if i == 1:
                    pe.wait_ge(kT_ready, B)
                nc.tensor.matmul(score_ps[i][:], qT[:, i * P:(i + 1) * P], kTs[:, i // TB], start=True,
                                 stop=True).then_inc(score_ready, 1)

            def prepare_mix():
                pe.wait_ge(mixwg_ready, 1)
                pe.wait_ge(be1_ready, 1)
                pe.wait_ge(center_ready, 1)
                nc.tensor.matmul(prep_ps[:, 0:D], centering[:], mixwg[:], start=True, stop=True)
                nc.tensor.matmul(prep_ps[:, D:2 * D], be1_wide[:], mixw1[:], start=True, stop=True).then_inc(prep_mm, 1)

            def turn_probs(i):
                pe.wait_ge(prob_ready, i + 1)
                if i == 0:
                    pe.wait_ge(kTs_ready, B)
                if i == 2:
                    pe.wait_ge(pT_act, 1)
                for j in range(KC):
                    last = turn(pT_ps[i][j // 2], j % 2, probs[:, i, j * P:(j + 1) * P])
                last.then_inc(pT_tp, 1)

            def attend(i):
                pe.wait_ge(pT_act, i + 1)
                pe.wait_ge(pT_dve, i + 1)
                for j in range(KC):
                    last = nc.tensor.matmul(attn_ps[i][:, 0:D], pT[:, i, j * P:(j + 1) * P], kv[:, i // TB, j],
                                            start=(j == 0), stop=(j == KC - 1))
                last.then_inc(attn_ready, 1)

            def turn_x1(i):
                pe.wait_ge(x1_ready, i + 1)
                turn(x1T_ps[i], 0, x1[:, i]).then_inc(x1T_tp, 1)

            def mix(i):
                pe.wait_ge(x1T_ready, i + 1)
                if i == 0:
                    pe.wait_ge(mixwc_ready, 1)
                    pe.wait_ge(be1_mixed_ready, 1)
                nc.tensor.matmul(mix_ps[:, i * D:(i + 1) * D], x1T[:, i], mixwc[:], start=True,
                                 stop=True).then_inc(mix_ready, 1)

            scores(0)
            scores(1)
            prepare_mix()
            scores(2)
            turn_probs(0)
            scores(3)
            turn_probs(1)
            attend(0)
            turn_probs(2)
            attend(1)
            turn_x1(0)
            turn_probs(3)
            attend(2)
            turn_x1(1)
            mix(0)
            attend(3)
            turn_x1(2)
            mix(1)
            turn_x1(3)
            mix(2)
            mix(3)
            keep_warm(WARM_NORMS)
            for b in range(B):
                for k in range(TB):
                    if b == 0:
                        pe.wait_ge(u2_dve, k + 1)
                    else:
                        pe.wait_ge(u2_act, k + 1)
                    last = turn(n2T_ps[b], k, u2[:, b * TB + k])
                last.then_inc(u2_tp, 1)
            pe.wait_ge(routw_in, 16)
            for i in range(T):
                pe.wait_ge(n2T_ready, i // TB + 1)
                nc.tensor.matmul(logit_ps[:, i * E:(i + 1) * E], n2T[:, i * P:(i + 1) * P], routw[:], start=True,
                                 stop=True).then_inc(logit_ready, 1)

            def three_passes(ps, high, low, moving_high, moving_low, start, stop):
                nc.tensor.matmul(ps, high, moving_high, start=start, stop=False)
                nc.tensor.matmul(ps, low, moving_high, start=False, stop=False)
                return nc.tensor.matmul(ps, high, moving_low, start=False, stop=stop)

            def hidden(n):
                e, w = n // FC, slice((n % FC) * P, (n % FC + 1) * P)
                if n == 0:
                    pe.wait_ge(n2l_ready, B)
                if n >= H_BANKS:
                    pe.wait_ge(hid_ready, n - H_BANKS + 1)
                if n % FC == 0:
                    pe.wait_ge(w1l_ready, e + 1)
                if n < NCH - 1:
                    three_passes(hid_ps[n % H_BANKS][:], w1h[:, e, w], w1l[:, e, w], n2h[:], n2l[:], True,
                                 True).then_inc(hid_mm, 1)
                    return
                for half in range(2):
                    pe.wait_ge(hid_ready, n + half - H_BANKS + 1)
                    three_passes(hid_ps[(n + half) % H_BANKS][:, 0:S], w1h[:, e, w], w1l[:, e, w], n2h[:, tok(half)],
                                 n2l[:, tok(half)], True, True).then_inc(hid_mm, 1)

            def project(n):
                e, c, buf = n // FC, n % FC, n % H_BUFS
                if c == 0:
                    pe.wait_ge(w2l_ready, e + 1)
                    if e >= 2:
                        pe.wait_ge(y_part_ready, e - 1)
                pe.wait_ge(hidl_ready, n + 1)
                if e < E - 1:
                    three_passes(y_ps[e % 2][:], w2h[:, e, c], w2l[:, e, c], hidh[:, buf], hidl[:, buf], c == 0,
                                 c == FC - 1).then_inc(hid_used, 1)
                    return
                for half in range(2):
                    if c == FC - 1:
                        pe.wait_ge(hidl_ready, n + half + 1)
                    last = three_passes(last_y_ps[half][:, 0:S], w2h[:, e, c], w2l[:, e, c], hidh[:, buf, tok(half)],
                                        hidl[:, buf, tok(half)], c == 0, c == FC - 1)
                    if c == FC - 1:
                        last.then_inc(last_y_ready, 1)
                if c < FC - 1:
                    last.then_inc(hid_used, 1)

            def turn_weights():
                pe.wait_ge(weight_ready, 1)
                for i in range(T):
                    last = nc.tensor.transpose(weightT_ps[0:E, i * P:(i + 1) * P], weight[:, i], ident[:])
                last.then_inc(weightT_tp, 1)

            def weighted_b2():
                pe.wait_ge(weightT_ready, 1)
                pe.wait_ge(b2_in, 16)
                nc.tensor.matmul(b2_ps[:], b2s[:], weightT[:], start=True, stop=True).then_inc(b2_ready, 1)

            for n in range(NCH + LAG - 1):
                if n < NCH:
                    hidden(n)
                if n >= LAG:
                    project(n - LAG)
                if n == LAG + 2:
                    turn_weights()
                if n == LAG + 3:
                    weighted_b2()
            pe.wait_ge(acc_ready, E - 1)
            for i in range(T):
                last = turn(accT_ps[i // TB], i % TB, acc[:, i * P:(i + 1) * P])
            last.then_inc(acc_tp, 1)
            project(NCH - 1)
            for half in range(2):
                pe.wait_ge(last_part_ready, half + 1)
                for k in range(TB):
                    i = half * TB + k
                    last = turn(last_yT_ps[half], k, y_part[:, (E - 1) % 2, i * P:(i + 1) * P])
                last.then_inc(last_yT_tp, 1)


_INS = ['x', 'ctx_1024', 'L0_ffn_g1', 'L0_ffn_be1', 'L0_ffn_mix_w', 'L0_ffn_mix_b', 'L0_ffn_g2', 'L0_ffn_be2',
        'L0_ffn_router_w', 'L0_ffn_w1', 'L0_ffn_b1', 'L0_ffn_w2', 'L0_ffn_b2']
_OUT = ((2, 256, 128), 'float32')


def kernel(**inputs):
    import numpy as _np
    import concourse.bacc as _bacc
    from concourse import mybir as _mybir
    from concourse.bass_utils import run_bass_kernel_spmd as _run

    nc = _bacc.Bacc("TRN2", target_bir_lowering=False, num_devices=1)
    arrays, args = {}, []
    for name in _INS:
        a = _np.ascontiguousarray(inputs[name])
        arrays[f"in_{name}_dram"] = a
        args.append(nc.dram_tensor(f"in_{name}_dram", a.shape, _mybir.dt.from_np(a.dtype), kind="ExternalInput").ap())
    args.append(nc.dram_tensor("out_dram", _OUT[0], _mybir.dt.from_np(_np.dtype(_OUT[1])), kind="ExternalOutput").ap())
    xattn_moe_kernel(nc, *args)
    r = _run(nc, [arrays], core_ids=[0])
    return r.results[0]["out_dram"]
```

```python
from contextlib import ExitStack

import concourse.bass as bass
from concourse import mybir

F32 = mybir.dt.float32
F32R = mybir.dt.float32r
BF16 = mybir.dt.bfloat16
I32 = mybir.dt.int32
ALU = mybir.AluOpType
ACT = mybir.ActivationFunctionType
AX_X = mybir.AxisListType.X

P = 128
EPS = 1e-5
TOP_K = 2
RSQRT_C = 0.9185584209116459
RSQRT_K = 0.27141074355784134 * (1 - 1.9e-7)
RSQRT_A1, RSQRT_A0 = -4.253164463819023, 5.291916161234017
RSQRT_B1, RSQRT_B0 = -0.9063260470190041, 1.713536060778617


def xattn_moe_kernel(nc: bass.Bass, x, ctx_kv, g1, be1, mix_w, mix_b, g2, be2, router_w, w1, b1, w2, b2, out):
    B, S, D = x.shape
    SK = ctx_kv.shape[1]
    E, _, F = w1.shape
    T = B * S // P
    TB = S // P
    KC = SK // P
    FC = F // P
    N = B * S
    Q_STEP = S // KC
    QR = B * KC
    assert D == P and KC == 4 and N == 512 and B == 2

    NCH = E * FC
    LAST = NCH - FC
    H_BANKS = 4
    H_BUFS = 4
    Y_BANKS = 3
    LAG = 6
    PT_SHARED = 3
    DVE_HIGH = 2
    ACT_HIGH = 4
    LAST_B2_AT = 13
    WEIGH_LAG = 10
    WARM_START = 10
    WARM_KEYS = 2
    WARM_NORMS = 20
    WARM_INPUTS = 3
    ROWS = NCH + 4 + E
    G1, BE1, G2, BE2 = (slice(NCH + i, NCH + i + 1) for i in range(4))

    x_tok = x.rearrange("b (n p) d -> p (b n) d", p=P)
    x_scale_rows = x.rearrange("b (j s) d -> (b j) s d", s=Q_STEP)[:, 0, :]
    out_tok = out.rearrange("b (n p) d -> p (b n) d", p=P)
    kv_tok = ctx_kv.rearrange("b (n p) d -> b p n d", p=P)
    w1_view = w1.rearrange("e d f -> d e f")
    w2_view = w2.rearrange("e (c p) d -> p e c d", p=P)
    weight_rows = nc.dram_tensor("weight_rows", [E, N], F32, kind="Internal").ap()

    with ExitStack() as stack:
        def sb(name, shape, dt=F32):
            return stack.enter_context(nc.sbuf_tensor(name, shape, dt))

        def sem(name):
            return stack.enter_context(nc.semaphore(name))

        bank = [stack.enter_context(nc.psum_tensor(f"bank{i}", [P, 512], F32)) for i in range(8)]
        scale_ps, kT_ps, prep_ps, qT_ps = bank[0], [bank[3], bank[4]], bank[0], [bank[1], bank[2], bank[5], bank[6]]
        score_ps = [bank[7], bank[3], bank[4], bank[5]]
        pT_ps = [(bank[1], bank[2]), (bank[6], bank[7]), (bank[3], bank[1]), (bank[4], bank[5])]
        attn_ps = [bank[2], bank[6], bank[3], bank[4]]
        x1T_ps, mix_ps = [bank[7], bank[1], bank[5], bank[2]], [bank[0], bank[1]]
        n2T_ps, logit_ps = [bank[6], bank[3]], [bank[4], bank[2]]
        more_hid_ps = {4: bank[4], 5: bank[2], 6: bank[3]}
        hid_ps, y_ps = [bank[5], bank[7], bank[1], bank[6]], [bank[0], bank[2], bank[4]]
        weightT_ps = bank[0]
        last_y_ps, accT_ps = [bank[2], bank[3], bank[4], bank[5]], bank[0]
        warm_ps = bank[7]

        ident = sb("ident", [P, P])
        centering = sb("centering", [P, P])
        xs = sb("xs", [P, T, D])
        xrows = sb("xrows", [QR, D])
        kv = sb("kv", [P, B, KC, D])
        const_rows = sb("const_rows", [ROWS, P])
        const_cols = sb("const_cols", [P, ROWS])
        mixw = sb("mixw", [P, D])
        mixw1 = sb("mixw1", [P, D])
        mixwg = sb("mixwg", [P, D])
        mixwc = sb("mixwc", [P, D])
        be1_wide = sb("be1_wide", [P, P])
        mixb = sb("mixb", [P, D])
        be1_mixed = sb("be1_mixed", [P, D])
        mix_const = sb("mix_const", [P, D])
        routw = sb("routw", [P, E])
        b2_last = sb("b2_last", [P, D])
        w1s = sb("w1s", [P, E, F])
        w2s = sb("w2s", [P, E, FC, D])
        w1h = sb("w1h", [P, E, F], F32R)
        w1l = sb("w1l", [P, E, F], F32R)
        w2h = sb("w2h", [P, E - 1, FC, D], F32R)
        w2l = sb("w2l", [P, E - 1, FC, D], F32R)

        stats = sb("stats", [P, T + 1, 6])
        meanvar = sb("meanvar", [P, T + 1, 2])
        var_eps = sb("var_eps", [P, 4 * T])
        guess = sb("guess", [P, 4 * T])
        guess_k = sb("guess_k", [P, 4 * T])
        square = sb("square", [P, 4 * T])
        ratio = sb("ratio", [P, 4 * T])
        quad_a = sb("quad_a", [P, 4 * T])
        quad_b = sb("quad_b", [P, 4 * T])
        rstd0 = sb("rstd0", [P, T + 1])
        rstd1 = sb("rstd1", [P, 2 * T])
        rstd2 = sb("rstd2", [P, T])
        shift1 = sb("shift1", [P, T])
        shift2 = sb("shift2", [P, TB])
        qn = sb("qn", [P, T, D])
        qrows = sb("qrows", [QR, D])
        qT = sb("qT", [P, N])
        scale_cols = sb("scale_cols", [P, QR])
        kvs = sb("kvs", [P, B, KC, D])
        kTs = sb("kTs", [P, B, SK])
        negmax = sb("negmax", [P, T])
        probs = sb("probs", [P, T, SK])
        probsum = sb("probsum", [P, T])
        probrec = sb("probrec", [P, T])
        pT = sb("pT", [P, T, SK])
        x1 = sb("x1", [P, T, D])
        x1T = sb("x1T", [P, T, P])
        x1s = sb("x1s", [P, T, D])
        zb = sb("zb", [P, T, D])
        x2 = sb("x2", [P, T, D])
        u2 = qn
        resid = sb("resid", [P, T, D])
        resid_acc = sb("resid_acc", [P, T, D])
        n2T = sb("n2T", [P, N])
        n2h = sb("n2h", [P, N], F32R)
        n2l = sb("n2l", [P, N], F32R)

        negtop = sb("negtop", [P, T])
        gate = sb("gate", [P, T, 2 * E])
        gate_rest = sb("gate_rest", [P, T, 2 * E])
        gate_sum = sb("gate_sum", [P, T])
        gate_rec = sb("gate_rec", [P, T])
        top8 = sb("top8", [P, T, 8])
        wanted = sb("wanted", [P, T, 8])
        picked = sb("picked", [P, T, E])
        weight = sb("weight", [P, T, E])
        weightT = sb("weightT", [T * E, P])
        weight_all = sb("weight_all", [P, E - 1, N])

        hid, y_part, acc = probs, pT[:, 0:2], pT[:, 2]
        hidh = sb("hidh", [P, H_BUFS, N], F32R)
        hidl = sb("hidl", [P, H_BUFS, N], F32R)
        result = sb("result", [P, T, D])
        warm = sb("warm", [P, 1])
        zeros = sb("zeros", [P, 512], BF16)

        xrows_in, x_in, kv_in = sem("xrows_in"), [sem(f"x_in{b}") for b in range(B)], [sem(f"kv_in{b}") for b in range(B)]
        rows_in, mixw_in, mixb_in, routw_in, b2_last_in = (sem(n) for n in ("rows_in", "mixw_in", "mixb_in", "routw_in", "b2_last_in"))
        w1_in = [sem(f"w1_in{e}") for e in range(E)]
        w2_in = [sem(f"w2_in{e}") for e in range(E)]
        pool_step, ident_ready, center_ready, mixw1_ready, mix_const_ready, warm_set = (
            sem(n) for n in ("pool_step", "ident_ready", "center_ready", "mixw1_ready", "mix_const_ready", "warm_set"))
        const_tp, const_ready, mixwg_ready, be1_ready, prep_mm, mixwc_ready, be1_mixed_ready = (
            sem(n) for n in ("const_tp", "const_ready", "mixwg_ready", "be1_ready", "prep_mm", "mixwc_ready", "be1_mixed_ready"))
        dve_step, zeros_ready = sem("dve_step"), sem("zeros_ready")
        rstd_rows_ready, rstd0_ready, qrows_ready, scale_tp, scale_ready, kvs_act, kvs_pool, kTs_tp, kTs_act, kTs_dve = (
            sem(n) for n in ("rstd_rows_ready", "rstd0_ready", "qrows_ready", "scale_tp", "scale_ready", "kvs_act", "kvs_pool",
                             "kTs_tp", "kTs_act", "kTs_dve"))
        kvs_dve, qn_ready, qT_tp, qT_ready = (sem(n) for n in ("kvs_dve", "qn_ready", "qT_tp", "qT_ready"))
        score_ready, negmax_ready, prob_ready, pT_tp, pT_act, pT_dve, attn_ready, x1_ready = (
            sem(n) for n in ("score_ready", "negmax_ready", "prob_ready", "pT_tp", "pT_act", "pT_dve", "attn_ready", "x1_ready"))
        x1T_tp, x1T_ready, mix_ready, x1s_ready, rstd1_ready, zb_ready, x2_ready = (
            sem(n) for n in ("x1T_tp", "x1T_ready", "mix_ready", "x1s_ready", "rstd1_ready", "zb_ready", "x2_ready"))
        rstd2_ready, u2_act, u2_dve, u2_tp, n2T_act, n2T_dve, n2h_act, n2h_dve, n2l_ready, resid_ready = (
            sem(n) for n in ("rstd2_ready", "u2_act", "u2_dve", "u2_tp", "n2T_act", "n2T_dve", "n2h_act", "n2h_dve", "n2l_ready", "resid_ready"))
        logit_ready, negtop_ready, gate_ready, pads_ready, weight_ready, weightT_tp, weightT_ready = (
            sem(n) for n in ("logit_ready", "negtop_ready", "gate_ready", "pads_ready", "weight_ready", "weightT_tp", "weightT_ready"))
        shift1_ready, shift2_ready = sem("shift1_ready"), sem("shift2_ready")
        weights_out, spread_in, resid_b2_ready = (
            sem("weights_out"), [sem(f"spread_in{e}") for e in range(E - 1)], sem("resid_b2_ready"))
        w1h_ready, w2h_ready, w1l_ready, w2l_ready = (sem(n) for n in ("w1h_ready", "w2h_ready", "w1l_ready", "w2l_ready"))
        hid_mm, hid_ready, first_hidh_ready, hidh_ready, hidl_ready, hid_used, y_part_ready, acc_ready = (
            sem(n) for n in ("hid_mm", "hid_ready", "first_hidh_ready", "hidh_ready", "hidl_ready", "hid_used", "y_part_ready", "acc_ready"))
        last_y_ready, acc_tp, resid_acc_ready, result_ready, out_done = (
            sem(n) for n in ("last_y_ready", "acc_tp", "resid_acc_ready", "result_ready", "out_done"))

        block = stack.enter_context(nc.Block())

        def tok(b):
            return slice(b * S, (b + 1) * S)

        def chunk_ps(n):
            return more_hid_ps.get(n, hid_ps[n % H_BANKS])

        def pair(b):
            return slice(b * TB, (b + 1) * TB)

        @block.sync
        def _(sp):
            sp.dma_start(xrows[:], x_scale_rows).then_inc(xrows_in, 16)
            for b in range(B):
                sp.dma_start(xs[:, b * TB:(b + 1) * TB], x_tok[:, b * TB:(b + 1) * TB]).then_inc(x_in[b], 16)
            for b in range(B):
                sp.dma_start(kv[:, b], kv_tok[b]).then_inc(kv_in[b], 16)
            sp.dma_start(const_rows[0:NCH, :], b1.rearrange("e (c p) -> (e c) p", p=P)).then_inc(rows_in, 16)
            sp.dma_start(const_rows[NCH + 4:ROWS, :], b2).then_inc(rows_in, 16)
            for i, v in enumerate((g1, be1, g2, be2)):
                sp.dma_start(const_rows[NCH + i:NCH + i + 1, :], v.rearrange("(o d) -> o d", o=1)).then_inc(rows_in, 16)
            sp.dma_start(mixw[:], mix_w).then_inc(mixw_in, 16)
            for e in range(E):
                sp.dma_start(w1s[:, e], w1_view[:, e]).then_inc(w1_in[e], 16)
                sp.dma_start(w2s[:, e], w2_view[:, e]).then_inc(w2_in[e], 16)
                if e == 0:
                    sp.dma_start(mixb[:], mix_b.partition_broadcast(P)).then_inc(mixb_in, 16)
                    sp.dma_start(routw[:], router_w).then_inc(routw_in, 16)
                    sp.dma_start(b2_last[:], b2[E - 1].partition_broadcast(P)).then_inc(b2_last_in, 16)
            sp.wait_ge(weightT_ready, 1)
            sp.dma_start(weight_rows.rearrange("e (t p) -> t e p", p=P), weightT[:]).then_inc(weights_out, 16)
            sp.wait_ge(weights_out, 16)
            for e in range(E - 1):
                sp.dma_start(weight_all[:, e, :], weight_rows[e, :].partition_broadcast(P)).then_inc(spread_in[e], 16)
            for half in range(2):
                sp.wait_ge(result_ready, (half + 1) * TB)
                sp.dma_start(out_tok[:, half * TB:(half + 1) * TB], result[:, half * TB:(half + 1) * TB]).then_inc(out_done, 16)
            sp.wait_ge(out_done, 32)

        @block.gpsimd
        def _(pool):
            nc.gpsimd.memset(ident[:], 0.0).then_inc(pool_step, 1)
            pool.wait_ge(pool_step, 1)
            nc.gpsimd.affine_select(out=ident[:], in_=ident[:], compare_op=ALU.not_equal, fill=1.0, base=0,
                                    pattern=[[-1, P]], channel_multiplier=1).then_inc(ident_ready, 1)
            pool.wait_ge(ident_ready, 1)
            nc.gpsimd.tensor_scalar(centering[:], ident[:], -1.0 / D, None, ALU.add).then_inc(center_ready, 1)
            pool.wait_ge(scale_ready, 1)
            pool.wait_ge(kv_in[1], 16)
            for j in range(KC // 2, KC):
                nc.gpsimd.tensor_scalar(kvs[:, 1, j], kv[:, 1, j], scale_cols[:, KC + j:KC + j + 1], None,
                                        ALU.mult).then_inc(kvs_pool, 1)
            pool.wait_ge(mixw_in, 16)
            nc.gpsimd.tensor_tensor(mixw1[:], mixw[:], ident[:], ALU.add).then_inc(mixw1_ready, 1)

            def low_parts(e):
                pool.wait_ge(w1h_ready, e + 1)
                nc.gpsimd.tensor_tensor(w1l[:, e], w1s[:, e], w1h[:, e].bitcast(F32), ALU.subtract).then_inc(w1l_ready, 1)
                if e == E - 1:
                    return
                pool.wait_ge(w2h_ready, e + 1)
                nc.gpsimd.tensor_tensor(w2l[:, e], w2s[:, e], w2h[:, e].bitcast(F32), ALU.subtract).then_inc(w2l_ready, 1)

            low_parts(0)
            pool.wait_ge(mixb_in, 16)
            pool.wait_ge(be1_mixed_ready, 1)
            nc.gpsimd.tensor_tensor(mix_const[:], be1_mixed[:], mixb[:], ALU.add).then_inc(mix_const_ready, 1)
            low_parts(1)
            for i in range(T):
                pool.wait_ge(x2_ready, i + 1)
                pool.wait_ge(x1s_ready, i + 1)
                nc.gpsimd.tensor_tensor(resid[:, i], x1s[:, i], x2[:, i], ALU.add).then_inc(resid_ready, 1)
            for e in range(2, ACT_HIGH):
                low_parts(e)
            for e in range(E - 2):
                if e + ACT_HIGH < E:
                    low_parts(e + ACT_HIGH)
                if e:
                    pool.wait_ge(y_part_ready, e + 1)
                    if e > 1:
                        pool.wait_ge(acc_ready, e - 1)
                    nc.gpsimd.tensor_tensor(acc, acc if e > 1 else y_part[:, 0], y_part[:, e % 2],
                                            ALU.add).then_inc(acc_ready, 1)

        @block.scalar
        def _(act):
            act.wait_ge(warm_set, 1)
            nc.scalar.activation(warm[:], warm[:], ACT.Exp)

            act.wait_ge(scale_tp, 1)
            nc.scalar.copy(scale_cols[:], scale_ps[:, 0:QR]).then_inc(scale_ready, 1)
            act.wait_ge(scale_ready, 1)
            act.wait_ge(kv_in[0], 16)
            for j in range(KC):
                nc.scalar.activation(kvs[:, 0, j], kv[:, 0, j], ACT.Copy, scale=scale_cols[:, j:j + 1]).then_inc(kvs_act, 1)

            act.wait_ge(kTs_tp, 1)
            nc.scalar.copy(kTs[:, 0], kT_ps[0][:]).then_inc(kTs_act, 1)

            def query_turned(i):
                act.wait_ge(qT_tp, i + 1)
                nc.scalar.copy(qT[:, i * P:(i + 1) * P], qT_ps[i][:, 0:P]).then_inc(qT_ready, 1)

            query_turned(0)
            query_turned(1)
            act.wait_ge(const_tp, 1)
            nc.scalar.copy(const_cols[:], prep_ps[:, 0:ROWS]).then_inc(const_ready, 1)
            act.wait_ge(const_ready, 1)
            act.wait_ge(mixw1_ready, 1)
            nc.scalar.activation(mixwg[:], mixw1[:], ACT.Copy, scale=const_cols[:, G1]).then_inc(mixwg_ready, 1)
            nc.scalar.activation(be1_wide[:], ident[:], ACT.Identity, bias=const_cols[:, BE1], scale=0.0).then_inc(be1_ready, 1)

            query_turned(2)
            query_turned(3)

            def softmax(i):
                act.wait_ge(negmax_ready, i + 1)
                nc.scalar.activation(probs[:, i], score_ps[i][:], ACT.Exp, bias=negmax[:, i:i + 1],
                                     accum_out=probsum[:, i:i + 1]).then_inc(prob_ready, 1)

            def half_pT(i):
                act.wait_ge(pT_tp, i + 1)
                if i >= PT_SHARED:
                    nc.scalar.copy(pT[:, i, 256:512], pT_ps[i][1][:, 0:256])
                nc.scalar.copy(pT[:, i, 0:256], pT_ps[i][0][:, 0:256]).then_inc(pT_act, 1)

            def x1_turned(i):
                act.wait_ge(x1T_tp, i + 1)
                nc.scalar.copy(x1T[:, i], x1T_ps[i][:, 0:P]).then_inc(x1T_ready, 1)

            def first_high(e):
                act.wait_ge(w1_in[e], 16)
                nc.scalar.copy(w1h[:, e], w1s[:, e]).then_inc(w1h_ready, 1)

            def second_high(e):
                act.wait_ge(w2_in[e], 16)
                nc.scalar.copy(w2h[:, e], w2s[:, e]).then_inc(w2h_ready, 1)

            softmax(0)
            softmax(1)
            half_pT(0)
            softmax(2)
            half_pT(1)
            act.wait_ge(w1h_ready, 1)
            first_high(1)
            softmax(3)
            half_pT(2)
            half_pT(3)
            act.wait_ge(prep_mm, 1)
            nc.scalar.copy(be1_mixed[:], prep_ps[:, D:2 * D]).then_inc(be1_mixed_ready, 1)
            nc.scalar.copy(mixwc[:], prep_ps[:, 0:D]).then_inc(mixwc_ready, 1)
            x1_turned(0)
            x1_turned(1)
            act.wait_ge(w2h_ready, 1)
            second_high(1)
            x1_turned(2)
            x1_turned(3)
            for e in range(2, ACT_HIGH):
                first_high(e)
                second_high(e)
            for i in range(T):
                act.wait_ge(shift1_ready, i // TB + 1)
                nc.scalar.activation(x1s[:, i], x1[:, i], ACT.Identity, bias=shift1[:, i:i + 1]).then_inc(x1s_ready, 1)
            act.wait_ge(shift2_ready, 1)
            nc.scalar.activation(u2[:, 1], x2[:, 1], ACT.Identity, bias=shift2[:, 1:2], scale=rstd2[:, 1:2]).then_inc(u2_act, 1)
            act.wait_ge(u2_tp, 1)
            nc.scalar.activation(n2T[:, tok(0)], n2T_ps[0][:, 0:S], ACT.Identity, bias=const_cols[:, BE2],
                                 scale=const_cols[:, G2]).then_inc(n2T_act, 1)
            act.wait_ge(n2T_act, 1)
            nc.scalar.copy(n2h[:, tok(0)], n2T[:, tok(0)]).then_inc(n2h_act, 1)
            act.wait_ge(pads_ready, 1)
            for i in range(T):
                b, k = i // TB, i % TB
                act.wait_ge(negtop_ready, b + 1)
                nc.scalar.activation(gate[:, i, 0:E], logit_ps[b][:, k * E:(k + 1) * E], ACT.Exp, bias=negtop[:, i:i + 1],
                                     accum_out=gate_sum[:, i:i + 1]).then_inc(gate_ready, 1)

            def silu(n):
                act.wait_ge(hid_mm, n + 1)
                if n >= H_BUFS:
                    act.wait_ge(hidl_ready, n - H_BUFS + 1)
                nc.scalar.activation(hid[:, n % H_BUFS], chunk_ps(n)[:], ACT.Silu,
                                     bias=const_cols[:, n:n + 1]).then_inc(hid_ready, 1)

            def high_part(n):
                act.wait_ge(hid_ready, n + 1)
                if n >= H_BUFS:
                    act.wait_ge(hid_used, n - H_BUFS + 1)
                nc.scalar.copy(hidh[:, n % H_BUFS], hid[:, n % H_BUFS]).then_inc(hidh_ready, 1)

            for n in range(NCH):
                silu(n)
                if DVE_HIGH < n <= LAST:
                    high_part(n - 1)

        @block.vector
        def _(dve):
            steps = [0]

            def step(ins):
                steps[0] += 1
                ins.then_inc(dve_step, 1)

            def settle():
                dve.wait_ge(dve_step, steps[0])

            last_step = {}

            def norm_step(cols, *instructions):
                for ins in instructions:
                    step(ins)
                last_step[cols.start] = steps[0]

            def after_last(cols):
                dve.wait_ge(dve_step, last_step[cols.start])

            def seed(c):
                after_last(c)
                norm_step(c, nc.vector.tensor_scalar(guess[:, c].bitcast(I32), var_eps[:, c].bitcast(I32), 1, 0x7FFFFFFF,
                                                     ALU.logical_shift_right, ALU.bitwise_xor))

            def squares(c):
                after_last(c)
                norm_step(c, nc.vector.scalar_tensor_tensor(out=square[:, c], in0=guess[:, c], scalar=2.0 ** -66,
                                                            in1=guess[:, c], op0=ALU.mult, op1=ALU.mult))
                norm_step(c, nc.vector.tensor_scalar(guess_k[:, c], guess[:, c], RSQRT_K * RSQRT_C ** 0.5 * 2.0 ** -65.5,
                                                     None, ALU.mult))

            def ratios(c):
                after_last(c)
                norm_step(c, nc.vector.scalar_tensor_tensor(out=ratio[:, c], in0=square[:, c], scalar=RSQRT_C * 2.0 ** -65,
                                                            in1=var_eps[:, c], op0=ALU.mult, op1=ALU.mult))

            def quadratics(c):
                after_last(c)
                norm_step(c, nc.vector.scalar_tensor_tensor(out=quad_b[:, c], in0=ratio[:, c], scalar=RSQRT_B1,
                                                            in1=ratio[:, c], op0=ALU.add, op1=ALU.mult))
                norm_step(c, nc.vector.scalar_tensor_tensor(out=quad_a[:, c], in0=ratio[:, c], scalar=RSQRT_A1,
                                                            in1=ratio[:, c], op0=ALU.add, op1=ALU.mult))

            def second_factor(c):
                after_last(c)
                norm_step(c, nc.vector.scalar_tensor_tensor(out=quad_b[:, c], in0=quad_b[:, c], scalar=RSQRT_B0,
                                                            in1=guess_k[:, c], op0=ALU.add, op1=ALU.mult))

            def finish(c, y, done):
                after_last(c)
                nc.vector.scalar_tensor_tensor(out=y, in0=quad_a[:, c], scalar=RSQRT_A0, in1=quad_b[:, c], op0=ALU.add,
                                               op1=ALU.mult).then_inc(done, 1)

            def first_high(e):
                dve.wait_ge(w1_in[e], 16)
                nc.vector.tensor_copy(w1h[:, e], w1s[:, e]).then_inc(w1h_ready, 1)

            def second_high(e):
                dve.wait_ge(w2_in[e], 16)
                nc.vector.tensor_copy(w2h[:, e], w2s[:, e]).then_inc(w2h_ready, 1)

            nc.vector.memset(zeros[:], 0.0).then_inc(zeros_ready, 1)
            nc.vector.memset(warm[:], 0.0).then_inc(warm_set, 1)
            nc.vector.memset(gate[:], -1.0).then_inc(pads_ready, 1)
            step(nc.vector.memset(wanted[:], -1.0))
            step(nc.vector.memset(meanvar[:], 1.0))

            rows, norm0 = slice(T, T + 1), slice(0, T)

            def x_stats(i):
                dve.wait_ge(x_in[i // TB], 16)
                step(nc.vector.bn_stats(stats[:, i], xs[:, i]))

            dve.wait_ge(xrows_in, 16)
            step(nc.vector.bn_stats(stats[0:QR, T], xrows[:]))
            settle()
            step(nc.vector.bn_aggr(meanvar[0:QR, T], stats[0:QR, T]))
            settle()
            norm_step(rows, nc.vector.tensor_scalar(var_eps[:, rows], meanvar[:, rows, 1], EPS, None, ALU.add))
            seed(rows)
            squares(rows)
            ratios(rows)
            x_stats(0)
            quadratics(rows)
            x_stats(1)
            second_factor(rows)
            x_stats(2)
            finish(rows, rstd0[:, rows], rstd_rows_ready)
            x_stats(3)
            dve.wait_ge(rstd_rows_ready, 1)
            nc.vector.tensor_scalar(qrows[:], xrows[:], meanvar[0:QR, T, 0:1], rstd0[0:QR, rows], ALU.subtract,
                                    ALU.mult).then_inc(qrows_ready, 1)
            settle()
            for i in range(T):
                step(nc.vector.bn_aggr(meanvar[:, i], stats[:, i]))
            settle()
            norm_step(norm0, nc.vector.tensor_scalar(var_eps[:, norm0], meanvar[:, norm0, 1], EPS, None, ALU.add))
            seed(norm0)
            squares(norm0)
            ratios(norm0)
            quadratics(norm0)
            second_factor(norm0)
            finish(norm0, rstd0[:, norm0], rstd0_ready)
            dve.wait_ge(rstd0_ready, 1)
            for i in range(T):
                nc.vector.tensor_scalar(qn[:, i], xs[:, i], meanvar[:, i, 0:1], rstd0[:, i:i + 1], ALU.subtract,
                                        ALU.mult).then_inc(qn_ready, 1)
                if i == 0:
                    dve.wait_ge(scale_ready, 1)
                    dve.wait_ge(kv_in[1], 16)
                    for j in range(KC // 2):
                        nc.vector.tensor_scalar(kvs[:, 1, j], kv[:, 1, j], scale_cols[:, KC + j:KC + j + 1], None,
                                                ALU.mult).then_inc(kvs_dve, 1)
            dve.wait_ge(kTs_tp, B)
            nc.vector.tensor_copy(kTs[:, 1], kT_ps[1][:]).then_inc(kTs_dve, 1)
            first_high(0)

            def row_max(i):
                dve.wait_ge(score_ready, i + 1)
                nc.vector.reduce_max(negmax[:, i:i + 1], score_ps[i][:], AX_X, negate=True).then_inc(negmax_ready, 1)

            def half_pT(i):
                dve.wait_ge(pT_tp, i + 1)
                nc.vector.tensor_copy(pT[:, i, 256:512], pT_ps[i][1][:, 0:256]).then_inc(pT_dve, 1)

            recip_step = {}

            def recip_sum(i):
                dve.wait_ge(prob_ready, i + 1)
                step(nc.vector.reciprocal(probrec[:, i:i + 1], probsum[:, i:i + 1]))
                recip_step[i] = steps[0]

            def attended(i):
                dve.wait_ge(dve_step, recip_step[i])
                dve.wait_ge(attn_ready, i + 1)
                nc.vector.scalar_tensor_tensor(out=x1[:, i], in0=attn_ps[i][:, 0:D], scalar=probrec[:, i:i + 1],
                                               in1=xs[:, i], op0=ALU.mult, op1=ALU.add).then_inc(x1_ready, 1)

            def x1_stats(i):
                dve.wait_ge(x1_ready, i + 1)
                step(nc.vector.bn_stats(stats[:, i], x1[:, i]))

            norm1 = [slice(b * 2 * TB, (b + 1) * 2 * TB) for b in range(B)]
            norm2 = [slice(2 * T + b * TB, 2 * T + (b + 1) * TB) for b in range(B)]

            def aggregate(c, b):
                settle()
                for i in range(b * TB, (b + 1) * TB):
                    step(nc.vector.bn_aggr(meanvar[:, i], stats[:, i]))
                last_step[c.start] = steps[0]

            def variances1(b):
                c = norm1[b]
                after_last(c)
                norm_step(c, nc.vector.tensor_scalar(var_eps[:, c.start:c.start + TB], meanvar[:, pair(b), 1], 1.0 + EPS,
                                                     EPS * EPS, ALU.mult, ALU.add))
                norm_step(c, nc.vector.tensor_scalar(var_eps[:, c.start + TB:c.stop], meanvar[:, pair(b), 1], EPS, None,
                                                     ALU.add))

            def variances2(b):
                c = norm2[b]
                after_last(c)
                norm_step(c, nc.vector.tensor_scalar(var_eps[:, c], meanvar[:, pair(b), 1], EPS, None, ALU.add))

            def shift(dst, rstd, b, done):
                nc.vector.scalar_tensor_tensor(out=dst[:, pair(b)], in0=meanvar[:, pair(b), 0], scalar=-1.0, in1=rstd,
                                               op0=ALU.mult, op1=ALU.mult).then_inc(done, 1)

            def shift1_of(b):
                c = norm1[b]
                dve.wait_ge(rstd1_ready, b + 1)
                shift(shift1, rstd1[:, c.start + TB:c.stop], b, shift1_ready)

            def make_zb(i):
                dve.wait_ge(rstd1_ready, i // TB + 1)
                if i == 0:
                    dve.wait_ge(mix_const_ready, 1)
                c = norm1[i // TB].start + TB + i % TB
                nc.vector.scalar_tensor_tensor(out=zb[:, i], in0=x1[:, i], scalar=rstd1[:, c:c + 1], in1=mix_const[:],
                                               op0=ALU.mult, op1=ALU.add).then_inc(zb_ready, 1)

            def make_x2(i):
                b, k = i // TB, i % TB
                dve.wait_ge(mix_ready, (b + 1) * TB)
                dve.wait_ge(zb_ready, i + 1)
                c = norm1[b].start + k
                nc.vector.scalar_tensor_tensor(out=x2[:, i], in0=mix_ps[b][:, k * D:(k + 1) * D], scalar=rstd1[:, c:c + 1],
                                               in1=zb[:, i], op0=ALU.mult, op1=ALU.add).then_inc(x2_ready, 1)

            def x2_stats(i):
                dve.wait_ge(x2_ready, i + 1)
                step(nc.vector.bn_stats(stats[:, i], x2[:, i]))

            def make_u2(i):
                dve.wait_ge(rstd2_ready, i // TB + 1)
                nc.vector.tensor_scalar(u2[:, i], x2[:, i], meanvar[:, i, 0:1], rstd2[:, i:i + 1], ALU.subtract,
                                        ALU.mult).then_inc(u2_dve, 1)

            def second_n2():
                dve.wait_ge(u2_tp, B)
                nc.vector.tensor_scalar(n2T[:, tok(1)], n2T_ps[1][:, 0:S], const_cols[:, G2], const_cols[:, BE2], ALU.mult,
                                        ALU.add).then_inc(n2T_dve, 1)
                dve.wait_ge(n2T_dve, 1)
                nc.vector.tensor_copy(n2h[:, tok(1)], n2T[:, tok(1)]).then_inc(n2h_dve, 1)

            def n2_low(b):
                if b == 0:
                    dve.wait_ge(n2h_act, 1)
                else:
                    dve.wait_ge(n2h_dve, 1)
                nc.vector.tensor_tensor(n2l[:, tok(b)], n2T[:, tok(b)], n2h[:, tok(b)].bitcast(F32),
                                        ALU.subtract).then_inc(n2l_ready, 1)

            def route_top(b):
                logits = logit_ps[b][:, 0:TB * E].rearrange("p (t e) -> p t e", e=E)
                dve.wait_ge(logit_ready, b + 1)
                nc.vector.reduce_max(negtop[:, pair(b)], logits, AX_X, negate=True).then_inc(negtop_ready, 1)

            row_max(0)
            row_max(1)
            second_high(0)
            row_max(2)
            half_pT(0)
            recip_sum(0)
            row_max(3)
            half_pT(1)
            recip_sum(1)
            attended(0)
            half_pT(2)
            recip_sum(2)
            attended(1)
            x1_stats(0)
            x1_stats(1)
            aggregate(norm1[0], 0)
            recip_sum(3)
            variances1(0)
            seed(norm1[0])
            attended(2)
            squares(norm1[0])
            ratios(norm1[0])
            x1_stats(2)
            quadratics(norm1[0])
            second_factor(norm1[0])
            attended(3)
            finish(norm1[0], rstd1[:, norm1[0]], rstd1_ready)
            x1_stats(3)
            shift1_of(0)
            aggregate(norm1[1], 1)
            make_zb(0)
            variances1(1)
            make_zb(1)
            seed(norm1[1])
            make_x2(0)
            squares(norm1[1])
            make_x2(1)
            ratios(norm1[1])
            x2_stats(0)
            quadratics(norm1[1])
            x2_stats(1)
            second_factor(norm1[1])
            aggregate(norm2[0], 0)
            finish(norm1[1], rstd1[:, norm1[1]], rstd1_ready)
            variances2(0)
            shift1_of(1)
            make_zb(2)
            seed(norm2[0])
            make_zb(3)
            squares(norm2[0])
            make_x2(2)
            ratios(norm2[0])
            make_x2(3)
            quadratics(norm2[0])
            x2_stats(2)
            second_factor(norm2[0])
            x2_stats(3)
            finish(norm2[0], rstd2[:, pair(0)], rstd2_ready)
            aggregate(norm2[1], 1)
            dve.wait_ge(rstd2_ready, 1)
            shift(shift2, rstd2[:, pair(0)], 0, shift2_ready)
            make_u2(0)
            variances2(1)
            seed(norm2[1])
            squares(norm2[1])
            ratios(norm2[1])
            quadratics(norm2[1])
            second_factor(norm2[1])
            finish(norm2[1], rstd2[:, pair(1)], rstd2_ready)
            make_u2(2)
            make_u2(3)
            n2_low(0)
            route_top(0)
            second_n2()
            route_top(1)
            n2_low(1)

            def route_largest():
                dve.wait_ge(gate_ready, T)
                for i in range(T):
                    step(nc.vector.max(top8[:, i], gate[:, i, 0:E]))
                settle()
                step(nc.vector.reciprocal(gate_rec[:], gate_sum[:]))
                step(nc.vector.tensor_copy(wanted[:, :, 0:TOP_K], top8[:, :, 0:TOP_K]))

            def route_pick():
                settle()
                for i in range(T):
                    step(nc.vector.match_replace(gate_rest[:, i], wanted[:, i], gate[:, i], 0.0))
                settle()
                step(nc.vector.tensor_tensor(picked[:], gate[:, :, 0:E], gate_rest[:, :, 0:E], ALU.subtract))

            def route_weights():
                settle()
                nc.vector.tensor_tensor(weight[:], picked[:], gate_rec[:].unsqueeze(2).broadcast_to([P, T, E]),
                                        ALU.mult).then_inc(weight_ready, 1)

            def route_turned():
                dve.wait_ge(weightT_tp, 1)
                nc.vector.tensor_copy(weightT[:], weightT_ps[0:T * E, 0:P]).then_inc(weightT_ready, 1)

            def low_part(n):
                if n < DVE_HIGH:
                    dve.wait_ge(hid_ready, n + 1)
                    nc.vector.tensor_copy(hidh[:, n], hid[:, n]).then_inc(first_hidh_ready, 1)
                    dve.wait_ge(first_hidh_ready, n + 1)
                else:
                    dve.wait_ge(hidh_ready, n - DVE_HIGH + 1)
                if n >= H_BUFS:
                    dve.wait_ge(hid_used, n - H_BUFS + 1)
                nc.vector.tensor_tensor(hidl[:, n % H_BUFS], hid[:, n % H_BUFS], hidh[:, n % H_BUFS].bitcast(F32),
                                        ALU.subtract).then_inc(hidl_ready, 1)

            def weigh(e):
                dve.wait_ge(hid_used, (e + 1) * FC)
                dve.wait_ge(spread_in[e], 16)
                if e >= 2:
                    dve.wait_ge(acc_ready, max(e - 2, 1))
                bias = NCH + 4 + e
                nc.vector.scalar_tensor_tensor(out=y_part[:, e % 2], in0=y_ps[e % Y_BANKS][:],
                                               scalar=const_cols[:, bias:bias + 1], in1=weight_all[:, e], op0=ALU.add,
                                               op1=ALU.mult).then_inc(y_part_ready, 1)
                if e == E - 2:
                    dve.wait_ge(acc_ready, e - 1)
                    dve.wait_ge(y_part_ready, e + 1)
                    nc.vector.tensor_tensor(acc, acc, y_part[:, e % 2], ALU.add).then_inc(acc_ready, 1)

            def last_b2(i):
                if i == 0:
                    dve.wait_ge(b2_last_in, 16)
                dve.wait_ge(resid_ready, i + 1)
                nc.vector.scalar_tensor_tensor(out=resid[:, i], in0=b2_last[:], scalar=weight[:, i, E - 1:E],
                                               in1=resid[:, i], op0=ALU.mult, op1=ALU.add).then_inc(resid_b2_ready, 1)

            route_largest()
            route_pick()
            route_weights()
            route_turned()
            weighing = {e * FC + WEIGH_LAG: e for e in range(E - 1)}
            for n in range(LAST):
                low_part(n)
                if n % FC == 3 and n // FC + ACT_HIGH < E:
                    first_high(n // FC + ACT_HIGH)
                    if n // FC + ACT_HIGH < E - 1:
                        second_high(n // FC + ACT_HIGH)
                if n in weighing:
                    weigh(weighing[n])
                if 0 <= n - LAST_B2_AT < T:
                    last_b2(n - LAST_B2_AT)
            for e in range(E - 1):
                if e * FC + WEIGH_LAG >= LAST:
                    weigh(e)
            dve.wait_ge(resid_b2_ready, T)
            dve.wait_ge(acc_tp, 1)
            nc.vector.tensor_tensor(resid_acc[:].rearrange("p t d -> p (t d)"), accT_ps[:],
                                    resid[:].rearrange("p t d -> p (t d)"), ALU.add).then_inc(resid_acc_ready, 1)
            dve.wait_ge(resid_acc_ready, 1)
            for i in range(T):
                dve.wait_ge(last_y_ready, i + 1)
                nc.vector.scalar_tensor_tensor(out=result[:, i], in0=last_y_ps[i][:, 0:D], scalar=weight[:, i, E - 1:E],
                                               in1=resid_acc[:, i], op0=ALU.mult, op1=ALU.add).then_inc(result_ready, 1)

        @block.tensor
        def _(pe):
            def keep_warm(products):
                for _ in range(products):
                    nc.tensor.matmul(warm_ps[:], zeros[:, 0:P], zeros[:], start=True, stop=True)

            def turn(dst, n, src):
                return nc.tensor.transpose(dst[:, n * P:(n + 1) * P], src, ident[:])

            pe.wait_ge(zeros_ready, 1)
            keep_warm(WARM_START)
            pe.wait_ge(ident_ready, 1)
            pe.wait_ge(qrows_ready, 1)
            nc.tensor.transpose(scale_ps[:, 0:QR], qrows[:], ident[0:QR, 0:QR]).then_inc(scale_tp, 1)

            def turn_keys(b):
                for j in range(KC):
                    if b == 0:
                        pe.wait_ge(kvs_act, j + 1)
                    elif j < KC // 2:
                        pe.wait_ge(kvs_dve, j + 1)
                    else:
                        pe.wait_ge(kvs_pool, j - KC // 2 + 1)
                    last = turn(kT_ps[b], j, kvs[:, b, j])
                last.then_inc(kTs_tp, 1)

            def turn_query(i):
                pe.wait_ge(qn_ready, i + 1)
                turn(qT_ps[i], 0, qn[:, i]).then_inc(qT_tp, 1)

            keep_warm(WARM_KEYS)
            turn_keys(0)
            turn_query(0)

            def turn_constants():
                pe.wait_ge(rows_in, 96)
                pe.wait_ge(scale_ready, 1)
                nc.tensor.transpose(prep_ps[:, 0:ROWS], const_rows[:], ident[0:ROWS, 0:ROWS]).then_inc(const_tp, 1)

            def scores(i):
                pe.wait_ge(qT_ready, i + 1)
                if i < TB:
                    pe.wait_ge(kTs_act, 1)
                else:
                    pe.wait_ge(kTs_dve, 1)
                nc.tensor.matmul(score_ps[i][:], qT[:, i * P:(i + 1) * P], kTs[:, i // TB], start=True,
                                 stop=True).then_inc(score_ready, 1)

            def prepare_mix():
                pe.wait_ge(mixwg_ready, 1)
                pe.wait_ge(be1_ready, 1)
                pe.wait_ge(center_ready, 1)
                nc.tensor.matmul(prep_ps[:, 0:D], centering[:], mixwg[:], start=True, stop=True)
                nc.tensor.matmul(prep_ps[:, D:2 * D], be1_wide[:], mixw1[:], start=True, stop=True).then_inc(prep_mm, 1)

            def turn_probs(i):
                pe.wait_ge(prob_ready, i + 1)
                if i == 2:
                    pe.wait_ge(pT_act, 1)
                for j in range(KC):
                    last = turn(pT_ps[i][j // 2], j % 2, probs[:, i, j * P:(j + 1) * P])
                last.then_inc(pT_tp, 1)

            def attend(i):
                pe.wait_ge(pT_act, i + 1)
                pe.wait_ge(pT_dve, min(i + 1, PT_SHARED))
                for j in range(KC):
                    last = nc.tensor.matmul(attn_ps[i][:, 0:D], pT[:, i, j * P:(j + 1) * P], kv[:, i // TB, j],
                                            start=(j == 0), stop=(j == KC - 1))
                last.then_inc(attn_ready, 1)

            def turn_x1(i):
                pe.wait_ge(x1_ready, i + 1)
                turn(x1T_ps[i], 0, x1[:, i]).then_inc(x1T_tp, 1)

            def mix(i):
                pe.wait_ge(x1T_ready, i + 1)
                if i == 0:
                    pe.wait_ge(mixwc_ready, 1)
                    pe.wait_ge(be1_mixed_ready, 1)
                nc.tensor.matmul(mix_ps[i // TB][:, (i % TB) * D:(i % TB + 1) * D], x1T[:, i], mixwc[:], start=True,
                                 stop=True).then_inc(mix_ready, 1)

            turn_constants()
            turn_keys(1)
            turn_query(1)
            scores(0)
            turn_query(2)
            turn_query(3)
            scores(1)
            scores(2)
            turn_probs(0)
            scores(3)
            turn_probs(1)
            attend(0)
            turn_probs(2)
            attend(1)
            turn_probs(3)
            attend(2)
            prepare_mix()
            attend(3)
            turn_x1(0)
            turn_x1(1)
            mix(0)
            turn_x1(2)
            mix(1)
            turn_x1(3)
            mix(2)
            mix(3)
            keep_warm(WARM_NORMS)

            def turn_u2(b):
                for k in range(TB):
                    i = b * TB + k
                    if i == 1:
                        pe.wait_ge(u2_act, 1)
                    else:
                        pe.wait_ge(u2_dve, max(i, 1))
                    last = turn(n2T_ps[b], k, u2[:, i])
                last.then_inc(u2_tp, 1)

            def logits(b):
                if b == 0:
                    pe.wait_ge(routw_in, 16)
                    pe.wait_ge(n2T_act, 1)
                else:
                    pe.wait_ge(n2T_dve, 1)
                for k in range(TB):
                    i = b * TB + k
                    last = nc.tensor.matmul(logit_ps[b][:, k * E:(k + 1) * E], n2T[:, i * P:(i + 1) * P], routw[:],
                                            start=True, stop=True)
                last.then_inc(logit_ready, 1)

            def three_passes(ps, high, low, moving_high, moving_low, start, stop, low_ready=None, count=0):
                nc.tensor.matmul(ps, high, moving_high, start=start, stop=False)
                nc.tensor.matmul(ps, low, moving_high, start=False, stop=False)
                if low_ready is not None:
                    pe.wait_ge(low_ready, count)
                return nc.tensor.matmul(ps, high, moving_low, start=False, stop=stop)

            def early_hidden(n, b):
                high, low, half = w1h[:, 0, n * P:(n + 1) * P], w1l[:, 0, n * P:(n + 1) * P], chunk_ps(n)[:, tok(b)]
                if n == 0:
                    if b == 0:
                        pe.wait_ge(n2h_act, 1)
                        pe.wait_ge(w1l_ready, 1)
                    else:
                        pe.wait_ge(n2h_dve, 1)
                last = three_passes(half, high, low, n2h[:, tok(b)], n2l[:, tok(b)], True, True, n2l_ready, b + 1)
                if b == B - 1:
                    last.then_inc(hid_mm, 1)

            def hidden(n):
                e, w = n // FC, slice((n % FC) * P, (n % FC + 1) * P)
                if n in more_hid_ps:
                    pe.wait_ge(gate_ready, T)
                else:
                    pe.wait_ge(hid_ready, n - H_BANKS + 1)
                if n % FC == 0:
                    pe.wait_ge(w1l_ready, e + 1)
                three_passes(chunk_ps(n)[:], w1h[:, e, w], w1l[:, e, w], n2h[:], n2l[:], True,
                             True).then_inc(hid_mm, 1)

            def project(n):
                e, c, buf = n // FC, n % FC, n % H_BUFS
                if c == 0:
                    pe.wait_ge(w2l_ready, e + 1)
                    if e >= Y_BANKS:
                        pe.wait_ge(y_part_ready, e - Y_BANKS + 1)
                if n == 0:
                    pe.wait_ge(weightT_ready, 1)
                if n < DVE_HIGH:
                    pe.wait_ge(first_hidh_ready, n + 1)
                else:
                    pe.wait_ge(hidh_ready, n - DVE_HIGH + 1)
                three_passes(y_ps[e % Y_BANKS][:], w2h[:, e, c], w2l[:, e, c], hidh[:, buf], hidl[:, buf], c == 0,
                             c == FC - 1, hidl_ready, n + 1).then_inc(hid_used, 1)

            def project_last(*chunks):
                pe.wait_ge(hid_ready, chunks[-1] + 1)
                if chunks[0] == LAST:
                    pe.wait_ge(w2_in[E - 1], 16)
                    pe.wait_ge(y_part_ready, E - 2)
                for i in range(T):
                    for n in chunks:
                        last = nc.tensor.matmul(last_y_ps[i][:, 0:D], hid[:, n % H_BUFS, i * P:(i + 1) * P],
                                                w2s[:, E - 1, n - LAST], start=(n == LAST), stop=(n == NCH - 1))
                    if chunks[-1] == NCH - 1:
                        last.then_inc(last_y_ready, 1)

            def turn_weights():
                pe.wait_ge(weight_ready, 1)
                nc.tensor.transpose(weightT_ps[0:T * E, 0:P], weight[:].rearrange("p t e -> p (t e)"),
                                    ident[:]).then_inc(weightT_tp, 1)

            turn_u2(0)
            keep_warm(WARM_INPUTS)
            logits(0)
            turn_u2(1)
            for n in range(2):
                early_hidden(n, 0)
            logits(1)
            for n in range(2, H_BANKS):
                early_hidden(n, 0)
            for n in range(H_BANKS):
                early_hidden(n, 1)
            for n in range(H_BANKS, NCH):
                hidden(n)
                if n == H_BANKS:
                    turn_weights()
                if n >= LAG:
                    project(n - LAG)
            for n in range(NCH - LAG, LAST):
                project(n)
            project_last(LAST)
            project_last(NCH - 3)
            pe.wait_ge(acc_ready, E - 2)
            for i in range(T):
                last = turn(accT_ps, i, acc[:, i * P:(i + 1) * P])
            last.then_inc(acc_tp, 1)
            project_last(NCH - 2, NCH - 1)


_INS = ['x', 'ctx_1024', 'L0_ffn_g1', 'L0_ffn_be1', 'L0_ffn_mix_w', 'L0_ffn_mix_b', 'L0_ffn_g2', 'L0_ffn_be2',
        'L0_ffn_router_w', 'L0_ffn_w1', 'L0_ffn_b1', 'L0_ffn_w2', 'L0_ffn_b2']
_OUT = ((2, 256, 128), 'float32')


def kernel(**inputs):
    import numpy as _np
    import concourse.bacc as _bacc
    from concourse import mybir as _mybir
    from concourse.bass_utils import run_bass_kernel_spmd as _run

    nc = _bacc.Bacc("TRN2", target_bir_lowering=False, num_devices=1)
    arrays, args = {}, []
    for name in _INS:
        a = _np.ascontiguousarray(inputs[name])
        arrays[f"in_{name}_dram"] = a
        args.append(nc.dram_tensor(f"in_{name}_dram", a.shape, _mybir.dt.from_np(a.dtype), kind="ExternalInput").ap())
    args.append(nc.dram_tensor("out_dram", _OUT[0], _mybir.dt.from_np(_np.dtype(_OUT[1])), kind="ExternalOutput").ap())
    xattn_moe_kernel(nc, *args)
    r = _run(nc, [arrays], core_ids=[0])
    return r.results[0]["out_dram"]
```
